# Optimizing a Trainium2 kernel written in Bass

```python
import numpy as np
import jax
import jax.numpy as jnp

def _softmax(x, axis=-1):
    return jax.nn.softmax(x, axis=axis)

def _gelu(x):
    return jax.nn.gelu(x, approximate=True)

def _silu(x):
    return jax.nn.silu(x)

def _sigmoid(x):
    return jax.nn.sigmoid(x)

def _layernorm(x, axis=-1, eps=1e-05):
    m = jnp.mean(x, axis=axis, keepdims=True)
    v = jnp.var(x, axis=axis, keepdims=True)
    return (x - m) / jnp.sqrt(v + eps)

def _scatter_add(tgt, idx, src, axis=0):
    return tgt.at[idx].add(src)

def _segment_sum(src, seg, n):
    return jax.ops.segment_sum(src, seg, n)
kernel_name = 'mk_vit_tower_d1_tok_img512_r4_d5c34d'

def setup_inputs(seed: int=0):
    np.random.seed(seed)
    _w = jnp.asarray

    def _rec_inputs():
        import jax
        import jax.numpy as jnp
        _rk = jax.random.key(seed)
        x = -0.000356955 + 1 * jax.random.normal(jax.random.fold_in(_rk, 1), (128, 3, 224, 224), jnp.float32)
        return x
    x = _rec_inputs()

    def _L0_tok_setup():
        import jax, jax.numpy as jnp
        import numpy as np
        key = jax.random.key(seed)
        k1, k2, k3 = jax.random.split(key, 3)
        B, C, H, W = (128, 3, 224, 224)
        E, p = (128, 16)
        K = C * p * p
        img = jax.random.normal(k1, (B, C, H, W), dtype=jnp.float32)
        w = jax.random.normal(k2, (E, K), dtype=jnp.float32) * (1.0 / np.sqrt(K))
        b = jax.random.normal(k3, (E,), dtype=jnp.float32)
        return {'img': img, 'w': w, 'b': b, 'patch_size': p}
    _L0_tok_all = _L0_tok_setup()
    _L0_tok_in = {k: v for k, v in _L0_tok_all.items() if k in ('w', 'b')}
    del _L0_tok_all

    def _L0_attn_setup():
        import jax, jax.numpy as jnp
        import numpy as np
        HEADS = 8
        DIM_HEAD = 64
        DIM = 128
        SCALE = DIM_HEAD ** (-0.5)
        BN_EPS = 1e-05
        key = jax.random.key(seed)
        ks = jax.random.split(key, 5)
        b, p = (8, 512)
        init = 0.05
        return {'x': jax.random.normal(ks[0], (b, p, DIM), jnp.float32), 'wq': jax.random.normal(ks[1], (HEADS, DIM_HEAD, DIM // HEADS), jnp.float32) * init, 'wk': jax.random.normal(ks[2], (HEADS, DIM_HEAD, DIM // HEADS), jnp.float32) * init, 'wv': jax.random.normal(ks[3], (HEADS, DIM_HEAD, DIM // HEADS), jnp.float32) * init, 'wo': jax.random.normal(ks[4], (DIM, HEADS * DIM_HEAD), jnp.float32) * init, 'gamma': jnp.ones((DIM,), jnp.float32), 'beta': jnp.zeros((DIM,), jnp.float32)}
    _L0_attn_all = _L0_attn_setup()
    _L0_attn_in = {k: v for k, v in _L0_attn_all.items() if k in ('wq', 'wk', 'wv', 'wo', 'gamma', 'beta')}
    del _L0_attn_all

    def _L0_ffn_setup():
        import jax, jax.numpy as jnp
        import numpy as np

        def _haar_dwt2(x):
            a = x[:, ::2, ::2]
            b = x[:, ::2, 1::2]
            c = x[:, 1::2, ::2]
            d = x[:, 1::2, 1::2]
            ll = (a + b + c + d) * 0.5
            lh = (a + b - c - d) * 0.5
            hl = (a - b + c - d) * 0.5
            hh = (a - b - c + d) * 0.5
            return (ll, lh, hl, hh)

        def _haar_idwt2(ll, lh, hl, hh):
            a = (ll + lh + hl + hh) * 0.5
            b = (ll + lh - hl - hh) * 0.5
            c = (ll - lh + hl - hh) * 0.5
            d = (ll - lh - hl + hh) * 0.5
            B, H2, W2 = ll.shape
            out = jnp.zeros((B, 2 * H2, 2 * W2), ll.dtype)
            out = out.at[:, ::2, ::2].set(a)
            out = out.at[:, ::2, 1::2].set(b)
            out = out.at[:, 1::2, ::2].set(c)
            out = out.at[:, 1::2, 1::2].set(d)
            return out

        def _interp_linear_last(x, m):
            n = x.shape[-1]
            pos = jnp.linspace(0.0, 1.0, m, dtype=x.dtype) * (n - 1)
            i0 = jnp.clip(jnp.floor(pos).astype(jnp.int32), 0, n - 2)
            w = pos - i0.astype(x.dtype)
            return x[..., i0] * (1.0 - w) + x[..., i0 + 1] * w
        key = jax.random.key(seed)
        k0, k1, k2 = jax.random.split(key, 3)
        b, f, c, hidden = (128, 64, 128, 512)
        x = jax.random.normal(k0, (b, f, c), dtype=jnp.float32)
        fc1_w = jax.random.normal(k1, (hidden, c), dtype=jnp.float32) * 0.02
        fc1_b = jnp.zeros((hidden,), dtype=jnp.float32)
        fc2_w = jax.random.normal(k2, (c // 2, hidden), dtype=jnp.float32) * 0.02
        fc2_b = jnp.zeros((c // 2,), dtype=jnp.float32)
        return {'x': x, 'fc1_w': fc1_w, 'fc1_b': fc1_b, 'fc2_w': fc2_w, 'fc2_b': fc2_b}
    _L0_ffn_all = _L0_ffn_setup()
    _L0_ffn_in = {k: v for k, v in _L0_ffn_all.items() if k in ('fc1_w', 'fc1_b', 'fc2_w', 'fc2_b')}
    del _L0_ffn_all
    return {'x': x, 'L0_tok_w': _L0_tok_in['w'], 'L0_tok_b': _L0_tok_in['b'], 'L0_attn_wq': _L0_attn_in['wq'], 'L0_attn_wk': _L0_attn_in['wk'], 'L0_attn_wv': _L0_attn_in['wv'], 'L0_attn_wo': _L0_attn_in['wo'], 'L0_attn_gamma': _L0_attn_in['gamma'], 'L0_attn_beta': _L0_attn_in['beta'], 'L0_ffn_fc1_w': _L0_ffn_in['fc1_w'], 'L0_ffn_fc1_b': _L0_ffn_in['fc1_b'], 'L0_ffn_fc2_w': _L0_ffn_in['fc2_w'], 'L0_ffn_fc2_b': _L0_ffn_in['fc2_b']}

def reference(x, L0_tok_w, L0_tok_b, L0_attn_wq, L0_attn_wk, L0_attn_wv, L0_attn_wo, L0_attn_gamma, L0_attn_beta, L0_ffn_fc1_w, L0_ffn_fc1_b, L0_ffn_fc2_w, L0_ffn_fc2_b):
    import jax
    import jax.numpy as jnp

    def _L0_tok_ref(img, w, b, patch_size):
        import jax, jax.numpy as jnp
        import numpy as np
        B, C, H, W = img.shape
        p = patch_size
        Hp, Wp = (H // p, W // p)
        S = Hp * Wp
        patches = img.reshape(B, C, Hp, p, Wp, p)
        patches = patches.transpose(0, 2, 4, 1, 3, 5).reshape(B, S, C * p * p)
        out = jnp.einsum('bsk,ek->bse', patches, w) + b
        return out

    def _L0_attn_ref(x, wq, wk, wv, wo, gamma, beta):
        import jax, jax.numpy as jnp
        import numpy as np
        HEADS = 8
        DIM_HEAD = 64
        DIM = 128
        SCALE = DIM_HEAD ** (-0.5)
        BN_EPS = 1e-05
        b, p, d = x.shape
        h, e = (HEADS, DIM_HEAD)
        xg = x.reshape(b, p, h, d // h)
        q = jnp.einsum('bphc,hec->bhpe', xg, wq)
        k = jnp.einsum('bphc,hec->bhpe', xg, wk)
        v = jnp.einsum('bphc,hec->bhpe', xg, wv)
        dots = jnp.einsum('bhie,bhje->bhij', q, k) * SCALE
        attn = jax.nn.softmax(dots, axis=-1)
        out = jnp.einsum('bhij,bhje->bhie', attn, v)
        out = out.transpose(0, 2, 1, 3).reshape(b, p, h * e)
        out = jnp.einsum('bpi,di->bpd', out, wo)
        mean = out.mean(axis=(0, 1))
        var = out.var(axis=(0, 1))
        out = (out - mean) * jax.lax.rsqrt(var + BN_EPS) * gamma + beta
        return jax.nn.relu(out)

    def _L0_ffn_ref(x, fc1_w, fc1_b, fc2_w, fc2_b):
        import jax, jax.numpy as jnp
        import numpy as np

        def _haar_dwt2(x):
            a = x[:, ::2, ::2]
            b = x[:, ::2, 1::2]
            c = x[:, 1::2, ::2]
            d = x[:, 1::2, 1::2]
            ll = (a + b + c + d) * 0.5
            lh = (a + b - c - d) * 0.5
            hl = (a - b + c - d) * 0.5
            hh = (a - b - c + d) * 0.5
            return (ll, lh, hl, hh)

        def _haar_idwt2(ll, lh, hl, hh):
            a = (ll + lh + hl + hh) * 0.5
            b = (ll + lh - hl - hh) * 0.5
            c = (ll - lh + hl - hh) * 0.5
            d = (ll - lh - hl + hh) * 0.5
            B, H2, W2 = ll.shape
            out = jnp.zeros((B, 2 * H2, 2 * W2), ll.dtype)
            out = out.at[:, ::2, ::2].set(a)
            out = out.at[:, ::2, 1::2].set(b)
            out = out.at[:, 1::2, ::2].set(c)
            out = out.at[:, 1::2, 1::2].set(d)
            return out

        def _interp_linear_last(x, m):
            n = x.shape[-1]
            pos = jnp.linspace(0.0, 1.0, m, dtype=x.dtype) * (n - 1)
            i0 = jnp.clip(jnp.floor(pos).astype(jnp.int32), 0, n - 2)
            w = pos - i0.astype(x.dtype)
            return x[..., i0] * (1.0 - w) + x[..., i0 + 1] * w
        b, f, c = x.shape
        ll, lh, hl, hh = _haar_dwt2(x)
        ll_up = _interp_linear_last(ll, c)
        h = jax.nn.gelu(jnp.einsum('bfc,hc->bfh', ll_up, fc1_w) + fc1_b, approximate=False)
        ll_new = jnp.einsum('bfh,oh->bfo', h, fc2_w) + fc2_b
        return _haar_idwt2(ll_new, lh, hl, hh)
    h = _L0_tok_ref(x, L0_tok_w, L0_tok_b, 16)
    h = h + _L0_attn_ref(_layernorm(h, axis=-1), L0_attn_wq, L0_attn_wk, L0_attn_wv, L0_attn_wo, L0_attn_gamma, L0_attn_beta)
    h = h + _L0_ffn_ref(_layernorm(h, axis=-1), L0_ffn_fc1_w, L0_ffn_fc1_b, L0_ffn_fc2_w, L0_ffn_fc2_b)
    return h

_drawn_inputs = setup_inputs


def setup_inputs(seed=0):
    import zlib

    import numpy as np

    out = dict(_drawn_inputs(seed))
    spreads = {'L0_attn_gamma': (1.0, 0.2),
     'L0_attn_beta': (0.0, 0.1),
     'L0_ffn_fc1_b': (0.0, 0.8),
     'L0_ffn_fc2_b': (0.0, 0.34)}
    factors = {'L0_ffn_fc1_w': 5.051, 'L0_ffn_fc2_w': 4.157}
    for name, (base, spread) in spreads.items():
        noise = np.random.default_rng([zlib.crc32(name.encode()), seed]).standard_normal(out[name].shape)
        drawn = base * np.exp(spread * noise) if base else spread * noise
        out[name] = jnp.asarray(drawn.astype(out[name].dtype))
    for name, factor in factors.items():
        out[name] = (out[name] * factor).astype(out[name].dtype)
    return out
```

```python
import numpy as np
import concourse.bass as bass
from concourse import mybir
from contextlib import ExitStack


F32 = mybir.dt.float32
F32R = mybir.dt.float32r
ALU = mybir.AluOpType
ACT = mybir.ActivationFunctionType
AX = mybir.AxisListType

B, CH, IMG, PATCH = 128, 3, 224, 16
GRID = IMG // PATCH
TOK = GRID * GRID
HALF = TOK // 2
E = 128
HEADS, DH = 8, 64
C = E // HEADS
PAIRS = HEADS // 2
SPLIT = 2
STEP = PATCH // SPLIT
XROWS = SPLIT * CH * PATCH
HID = 512
HT = HID // 128
EPS = 1e-5
RING = 4
UNITS = 8
AUG = 2 * C


class Image:

    def __init__(self, block, place):
        self.fixed = isinstance(block, int)
        self.block = block + place // RING
        self.place = place % RING
        self.index = self.block * RING + self.place

    def plus(self, d):
        return Image(self.block, self.place + d)

    def exists(self, count=B):
        return not self.fixed or 0 <= self.index < count

    def after(self, d):
        return not self.fixed or self.index >= d

    def total(self, per, c):
        return self.block * (RING * per) + (self.place * per + c)

    def turn(self, slots, per):
        return self.block * (RING // slots * per) + (self.place // slots + 1) * per


def vit_layer(nc, x, tok_w, tok_b, wq, wk, wv, wo, gamma, beta, fc1_w, fc1_b, fc2_w, fc2_b,
              c_ident, c_center, c_heads, c_interp, c_pair, out):
    ctx = ExitStack()
    with ctx:
        lifetime = [ctx]

        def sb(name, shape, dt=F32):
            return lifetime[0].enter_context(nc.sbuf_tensor(name, shape, dt))

        def sem(name):
            return ctx.enter_context(nc.semaphore(name))

        ctx.enter_context(nc.allow_non_contiguous_dma("short rows of small weights"))
        h_dram = nc.dram_tensor("h_spill", [B // RING, RING, E, TOK], F32, kind="Internal").ap()

        ident = sb("ident", [128, 128])
        center = sb("center", [E, E])
        headmask = sb("headmask", [E, E])
        interp = sb("interp", [E, E])
        pairsum = sb("pairsum", [E, E])
        w_embed = sb("w_embed", [XROWS, STEP, E])
        b_embed = sb("b_embed", [E, 1])
        w_q = sb("w_q", [E, E])
        w_out = sb("w_out", [E, E])
        w_ffn1 = sb("w_ffn1", [E, HID])
        w_ffn2 = sb("w_ffn2", [128, HT, E])
        b_ffn1 = sb("b_ffn1", [128, HT])
        b_ffn2 = sb("b_ffn2", [1, E])
        b_ffn2_raw = sb("b_ffn2_raw", [1, E // 2])
        ones = sb("ones", [1, HALF])
        gam = sb("gam", [E, 1])
        bet = sb("bet", [E, 1])
        oT = sb("oT", [E, B * TOK])
        ostats = sb("ostats", [E, B * 6])
        bn = sb("bn", [E, 6])

        minus_half = sb("minus_half", [128, 4])

        phase1 = ctx.enter_context(ExitStack())
        lifetime[0] = phase1
        xin = [sb(f"xin{k}", [XROWS, GRID, IMG]) for k in range(2)]
        hT = [sb(f"hT{k}", [E, TOK]) for k in range(RING)]
        st1 = sb("st1", [HALF, 2, 6])
        mv1 = sb("mv1", [HALF, 2, 2])
        ve1 = sb("ve1", [HALF, 2])
        rs1 = sb("rs1", [HALF, 2])
        xn = [sb(f"xn{k}", [HALF, 2, E]) for k in range(2)]
        qf = [sb(f"qf{k}", [HALF, 2, E]) for k in range(2)]
        kst = [sb(f"kst{k}", [HALF, 2, HEADS, 4 * C]) for k in range(2)]
        qst = [sb(f"qst{k}", [HALF, 2, HEADS, 4 * C]) for k in range(2)]
        vpad = [sb(f"vpad{k}", [HALF, 2, HEADS, 2 * C]) for k in range(RING)]
        kT = [sb(f"kT{k}", [128, PAIRS, TOK], F32R) for k in range(RING)]
        qT = [sb(f"qT{k}", [128, PAIRS, TOK], F32R) for k in range(RING)]
        rmax = [sb(f"rmax{k}", [HALF, 2, HEADS]) for k in range(2)]
        negm = sb("negm", [HALF, 2, HEADS])
        mT = [sb(f"mT{k}", [HEADS, TOK], F32R) for k in range(2)]
        probs = [sb(f"probs{k}", [HALF, 4, TOK]) for k in range(2)]
        ysb = sb("ysb", [128, 2, TOK])
        rden = sb("rden", [HALF, 4 * 4])
        yn = sb("yn", [HALF, 2, E])
        ynT = sb("ynT", [E, TOK])

        bank = [ctx.enter_context(nc.psum_tensor(f"bank{k}", [128, 512], F32)) for k in range(8)]
        P_EMB, P_TOK, P_MIX, P_Y = bank[0], bank[1], bank[2], bank[3]
        P_MAX, P_SC = bank[4:6], bank[6:8]

        settled = sem("settled")
        w_loaded = sem("w_loaded")
        pads_set = sem("pads_set")
        rows_ready = sem("rows_ready")
        setup_pe = sem("setup_pe")
        setup_dve = sem("setup_dve")
        x_loaded = [sem(f"x_loaded{k}") for k in range(2)]
        h_spilled = [sem(f"h_spilled{k}") for k in range(RING)]
        shift_put = [sem(f"shift_put{k}") for k in range(RING)]
        embedded = sem("embedded")
        h_ready = sem("h_ready")
        tokens_out = sem("tokens_out")
        stats_in = sem("stats_in")
        mv_ready = sem("mv_ready")
        ve1_ready = sem("ve1_ready")
        rstd_ready = sem("rstd_ready")
        xn_ready = sem("xn_ready")
        qf_ready = sem("qf_ready")
        khi_ready = sem("khi_ready")
        kst_ready = sem("kst_ready")
        qhi_ready = sem("qhi_ready")
        qst_ready = sem("qst_ready")
        v_ready = sem("v_ready")
        k_turned = sem("k_turned")
        q_turned = sem("q_turned")
        kT_ready = sem("kT_ready")
        qT_ready = sem("qT_ready")
        max_scored = sem("max_scored")
        max_taken = sem("max_taken")
        negm_ready = sem("negm_ready")
        m_turned = sem("m_turned")
        mT_ready = sem("mT_ready")
        scored = sem("scored")
        probs_ready = sem("probs_ready")
        weighted = sem("weighted")
        y_ready = sem("y_ready")
        y_turned = sem("y_turned")
        rden_ready = sem("rden_ready")
        yn_ready = sem("yn_ready")
        yn_turned = sem("yn_turned")
        ynT_ready = sem("ynT_ready")
        projected = sem("projected")
        o_ready = sem("o_ready")
        ostat_ready = sem("ostat_ready")
        bn_ready = sem("bn_ready")

        raw = oT[:, 0:768]
        raw_wo = oT[:, 768:1280]
        raw_fc1 = oT[:, 1280:1792].rearrange("p (k m) -> p k m", k=HT)
        raw_fc2 = oT[0:E // 2, 1792:2304]
        raw_wq = oT[0:DH, 2304:2432].rearrange("p (h c) -> p h c", h=HEADS)
        raw_wk = oT[0:DH, 2432:2560].rearrange("p (h c) -> p h c", h=HEADS)
        wv_bd = oT[:, 2560:3072].rearrange("p (t c) -> p t c", t=HT)
        woT = oT[:, 3072:3584]
        w1T = oT[:, 3584:4096]
        m_sb = oT[:, 4096:4224]
        raw_rows = oT[:, 4224:4992].rearrange("e (s g k) -> e s g k", s=STEP, g=SPLIT)
        N_W = 16 * (16 + HEADS)

        xv = x.rearrange("b c (hp py) w -> b c py hp w", py=PATCH)

        def settle(eng):
            eng.sem_inc(settled, 1)

        def period_range(eng, period, lead, tail):
            for t in range(-lead, RING):
                period(Image(0, t))
            with eng.Fori(1, B // RING - 2) as i:
                for k in range(RING):
                    period(Image(i, k))
            for t in range(B - 2 * RING, B + tail):
                period(Image(0, t))

        block1 = nc.Block()
        with block1 as block:

            @block.sync
            def _(sp):
                for dst, src in ((ident, c_ident), (center, c_center), (headmask, c_heads),
                                 (interp, c_interp), (pairsum, c_pair)):
                    sp.dma_start(dst[:, :], src).then_inc(w_loaded, 16)
                sp.dma_start(raw, tok_w).then_inc(w_loaded, 16)
                for dst, src in ((b_embed, tok_b), (gam, gamma), (bet, beta)):
                    sp.dma_start(dst[:, :], src.rearrange("(p a) -> p a", a=1)).then_inc(w_loaded, 16)
                sp.dma_start(raw_wq, wq.rearrange("h e c -> e h c")).then_inc(w_loaded, 16)
                sp.dma_start(raw_wk, wk.rearrange("h e c -> e h c")).then_inc(w_loaded, 16)
                sp.dma_start(raw_wo, wo).then_inc(w_loaded, 16)
                sp.dma_start(raw_fc1, fc1_w.rearrange("(k p) m -> p k m", p=128)).then_inc(w_loaded, 16)
                sp.dma_start(raw_fc2, fc2_w).then_inc(w_loaded, 16)
                sp.dma_start(b_ffn1[:, :], fc1_b.rearrange("(k p) -> p k", p=128)).then_inc(w_loaded, 16)
                sp.dma_start(b_ffn2_raw[:, :], fc2_b.rearrange("(a n) -> a n", a=1)).then_inc(w_loaded, 16)
                sp.wait_ge(pads_set, 1)
                for h in range(HEADS):
                    sp.dma_start(wv_bd[DH * (h % 2):DH * (h % 2) + DH, h // 2, C * h:C * h + C],
                                 wv[h, :, :]).then_inc(w_loaded, 16)

                def load(img):
                    k = img.place % 2
                    if img.after(2):
                        sp.wait_ge(embedded, img.plus(-2).total(1, 1))
                    settle(sp)
                    for g in range(SPLIT):
                        for c in range(CH):
                            p, n = (g * CH + c) * PATCH, IMG - g * STEP
                            sp.dma_start(xin[k][p:p + PATCH, :, 0:n],
                                         xv[img.index, c, :, :, g * STEP:IMG]).then_inc(x_loaded[k], 16)

                def period(t):
                    a = t.plus(4)
                    if a.exists():
                        sp.wait_ge(h_ready, a.total(1, 1))
                        settle(sp)
                        sp.dma_start(h_dram[a.block, a.place], hT[a.place][:, :]).then_inc(h_spilled[a.place], 16)
                    a = t.plus(1)
                    if a.exists():
                        sp.wait_ge(mT_ready, a.total(1, 1))
                        settle(sp)
                        for e in range(2):
                            sp.dma_start(qT[a.place][64 * e + AUG:64 * e + AUG + 1, :, :].bitcast(F32),
                                         mT[a.place % 2][PAIRS * e:PAIRS * e + PAIRS, :].bitcast(F32))\
                              .then_inc(shift_put[a.place], 16)
                    a = t.plus(7)
                    if a.exists():
                        load(a)

                period_range(sp, period, 7, 0)
                for k in range(RING):
                    sp.wait_ge(h_spilled[k], 16 * (B // RING))

            @block.gpsimd
            def _(pool):
                pool.memset(wv_bd[:, :, :], 0.0).then_inc(pads_set, 1)
                pool.memset(ones[:, :], 1.0).then_inc(pads_set, 1)
                pool.memset(minus_half[:, :], -0.5).then_inc(pads_set, 1)
                for k in range(2):
                    pool.memset(kst[k][:, :, :, :], 0.0).then_inc(pads_set, 1)
                    pool.memset(qst[k][:, :, :, :], 0.0).then_inc(pads_set, 1)
                for k in range(RING):
                    pool.memset(vpad[k][:, :, :, :], 0.0).then_inc(pads_set, 1)
                pool.wait_ge(pads_set, 3 + 4 + RING)
                for k in range(2):
                    pool.memset(kst[k][:, :, :, AUG:AUG + 1], 1.0).then_inc(pads_set, 1)
                for k in range(RING):
                    pool.memset(vpad[k][:, :, :, C:C + 1], 1.0).then_inc(pads_set, 1)
                pool.wait_ge(pads_set, 3 + 4 + RING + 2 + RING)

                def period(t):
                    a = t.plus(1)
                    if a.exists():
                        pool.wait_ge(max_taken, a.total(UNITS, UNITS))
                        if a.after(1):
                            pool.wait_ge(m_turned, a.total(1, 0))
                        settle(pool)
                        pool.tensor_scalar(negm[:, :, :].bitcast(F32R), rmax[a.place % 2][:, :, :], -1.0,
                                           None, ALU.mult).then_inc(negm_ready, 1)
                    a = t.plus(3)
                    if a.exists():
                        s = a.place % 2
                        pool.wait_ge(qf_ready, a.total(2, 2))
                        if a.after(2):
                            pool.wait_ge(q_turned, a.plus(-2).total(2, 2))
                        settle(pool)
                        for it in range(2):
                            src = qf[s][:, it, :].rearrange("p (h c) -> p h c", c=C)
                            pool.tensor_scalar(qst[s][:, it, :, 0:C].bitcast(F32R), src, 1.0, None,
                                               ALU.mult).then_inc(qhi_ready, 1)
                            pool.tensor_scalar(qst[s][:, it, :, 3 * C:4 * C].bitcast(F32R), src, 1.0, None,
                                               ALU.mult).then_inc(qhi_ready, 1)
                        pool.wait_ge(qhi_ready, a.total(4, 4))
                        pool.tensor_tensor(qst[s][:, :, :, C:2 * C].bitcast(F32R),
                                           qf[s][:, :, :].rearrange("p t (h c) -> p t h c", c=C),
                                           qst[s][:, :, :, 0:C], ALU.subtract).then_inc(qst_ready, 1)
                        pool.wait_ge(xn_ready, a.total(2, 2))
                        if a.after(4):
                            pool.wait_ge(weighted, a.plus(-4).total(4, 4))
                        settle(pool)
                        pool.tensor_scalar(vpad[a.place][:, :, :, 0:C],
                                           xn[s][:, :, :].rearrange("p t (h c) -> p t h c", c=C), 1.0, None,
                                           ALU.mult).then_inc(v_ready, 1)
                    a = t.plus(4)
                    if a.exists():
                        s = a.place % 2
                        pool.wait_ge(mv_ready, a.total(2, 2))
                        if a.after(1):
                            pool.wait_ge(qf_ready, a.total(2, 0))
                        settle(pool)
                        pool.tensor_scalar(ve1[:, :], mv1[:, :, 1], EPS, None, ALU.add).then_inc(ve1_ready, 1)
                        pool.wait_ge(ve1_ready, a.total(1, 1))
                        pool.tensor_tensor(rs1[:, :], ve1[:, :], minus_half[0:HALF, 0:2], ALU.pow)\
                            .then_inc(rstd_ready, 1)
                        pool.wait_ge(xn_ready, a.total(2, 2))
                        if a.after(2):
                            pool.wait_ge(k_turned, a.plus(-2).total(2, 2))
                        settle(pool)
                        for it in range(2):
                            src = xn[s][:, it, :].rearrange("p (h c) -> p h c", c=C)
                            for q in range(2):
                                pool.tensor_scalar(kst[s][:, it, :, C * q:C * q + C].bitcast(F32R), src, 1.0,
                                                   None, ALU.mult).then_inc(khi_ready, 1)
                        pool.wait_ge(khi_ready, a.total(4, 4))
                        pool.tensor_tensor(kst[s][:, :, :, 3 * C:4 * C].bitcast(F32R),
                                           xn[s][:, :, :].rearrange("p t (h c) -> p t h c", c=C),
                                           kst[s][:, :, :, 0:C], ALU.subtract).then_inc(kst_ready, 1)

                period_range(pool, period, 7, 0)

            @block.scalar
            def _(act):
                act.wait_ge(w_loaded, N_W)

                def period(t):
                    for u in range(UNITS):
                        a = t.plus(4)
                        if u == 0 and a.exists():
                            act.wait_ge(embedded, a.total(1, 1))
                            if a.after(RING):
                                act.wait_ge(h_spilled[a.place], a.plus(-RING).turn(RING, 16))
                                act.wait_ge(tokens_out, a.plus(-RING).total(1, 1))
                            nc.scalar.activation(hT[a.place][:, :], P_EMB[:, 0:TOK], ACT.Identity,
                                                 bias=b_embed[:, 0:1]).then_inc(h_ready, 1)
                        a = t.plus(-1)
                        if u == 0 and a.exists():
                            act.wait_ge(weighted, a.total(4, 4))
                            if a.after(1):
                                act.wait_ge(y_turned, a.total(1, 0))
                            nc.scalar.activation(ysb[:, :, :], P_Y[:, 0:2 * TOK], ACT.Copy).then_inc(y_ready, 1)
                        a = t.plus(3)
                        if u in (1, 2) and a.exists():
                            act.wait_ge(k_turned, a.total(2, u))
                            nc.scalar.activation(kT[a.place][:, 2 * u - 2:2 * u, :], P_MIX[:, 0:2 * TOK],
                                                 ACT.Copy).then_inc(kT_ready, 1)
                        if u in (3, 6) and a.exists():
                            v = u // 3 - 1
                            act.wait_ge(q_turned, a.total(2, v + 1))
                            nc.scalar.activation(qT[a.place][:, 2 * v:2 * v + 2, :], P_MIX[:, 0:2 * TOK],
                                                 ACT.Copy).then_inc(qT_ready, 1)
                        a = t.plus(-1)
                        if u == 4 and a.exists():
                            act.wait_ge(yn_turned, a.total(1, 1))
                            nc.scalar.activation(ynT[:, :], P_MIX[:, 0:TOK], ACT.Copy).then_inc(ynT_ready, 1)
                        if u == 5 and a.exists():
                            act.wait_ge(projected, a.total(1, 1))
                            nc.scalar.activation(oT[:, bass.ds(a.index * TOK, TOK)], P_MIX[:, 0:TOK],
                                                 ACT.Copy).then_inc(o_ready, 1)
                        if t.exists():
                            act.wait_ge(scored, t.total(UNITS, u + 1))
                            if u % 2 == 0 and (u >= 4 or t.after(1)):
                                act.wait_ge(weighted, t.total(4, u // 2 - 1))
                            nc.scalar.activation(probs[u // 2 % 2][:, u % 2::2, :],
                                                 P_SC[u % 2][0:HALF, 0:2 * TOK], ACT.Exp)\
                                .then_inc(probs_ready, 1)

                period_range(act, period, 5, 1)

            @block.vector
            def _(dve):
                def turned(v, dst, src):
                    dve.wait_ge(setup_pe, v)
                    nc.vector.tensor_copy(dst, src).then_inc(setup_dve, 1)

                dve.wait_ge(w_loaded, N_W)
                dve.wait_ge(pads_set, 3)
                nc.vector.tensor_copy(raw_rows, raw.rearrange("e (cp g s) -> e s g cp", g=SPLIT, s=STEP))\
                    .then_inc(rows_ready, 1)
                for g in range(2):
                    turned(g + 1, w_embed[:, 4 * g:4 * g + 4, :], bank[g][0:XROWS, :])
                turned(3, woT, bank[2][:, :])
                turned(4, w1T, bank[3][:, :])
                dve.wait_ge(setup_pe, 5)
                for k in range(HT):
                    for d in range(2):
                        nc.vector.tensor_scalar(w_ffn2[:, k, d::2], bank[4][:, 64 * k:64 * k + 64], 0.5, None,
                                                ALU.mult).then_inc(setup_dve, 1)
                for d in range(2):
                    nc.vector.tensor_scalar(b_ffn2[:, d::2], b_ffn2_raw[:, :], 0.5, None, ALU.mult)\
                        .then_inc(setup_dve, 1)
                dve.wait_ge(setup_pe, 6)
                nc.vector.tensor_tensor(m_sb, bank[5][:, 0:E], headmask[:, :], ALU.mult).then_inc(setup_dve, 1)
                turned(7, w_out[:, :], bank[6][:, 0:E])
                turned(8, w_ffn1[:, :], bank[7][:, :])
                turned(9, w_q[:, :], bank[5][:, 0:E])

                def period(t):
                    for u in range(UNITS):
                        a = t.plus(2)
                        if a.exists():
                            dve.wait_ge(max_scored, a.total(UNITS, u + 1))
                            if u == 0 and a.after(2):
                                dve.wait_ge(negm_ready, a.plus(-2).total(1, 1))
                            it, first = u // PAIRS, PAIRS * (u % 2) + 2 * (u // 2 % 2)
                            nc.vector.reduce_max(
                                rmax[a.place % 2][:, it, first:first + 2],
                                P_MAX[u % 2][0:HALF, 0:2 * TOK].rearrange("p (q j) -> p q j", q=2), AX.X)\
                                .then_inc(max_taken, 1)
                        a = t.plus(1)
                        if u == 1 and a.exists():
                            dve.wait_ge(m_turned, a.total(1, 1))
                            if a.after(2):
                                dve.wait_ge(shift_put[(a.place + 2) % RING], a.plus(-2).turn(RING, 32))
                            nc.vector.tensor_copy(mT[a.place % 2][:, :], P_TOK[0:HEADS, 0:TOK])\
                                .then_inc(mT_ready, 1)
                        a = t.plus(-1)
                        if u == 2 and a.exists():
                            groups = P_TOK[0:HALF, :].rearrange("p (n c) -> p n c", c=2 * C)
                            dve.wait_ge(y_turned, a.total(1, 1))
                            nc.vector.reciprocal(rden[:, :], groups[:, :, C]).then_inc(rden_ready, 1)
                            dve.wait_ge(rden_ready, a.total(1, 1))
                            if a.after(1):
                                dve.wait_ge(yn_turned, a.total(1, 0))
                            nc.vector.tensor_tensor(
                                yn[:, :, :].rearrange("p t (h c) -> p (t h) c", c=C), groups[:, :, 0:C],
                                rden[:, :].unsqueeze(2).to_broadcast([HALF, 16, C]), ALU.mult)\
                                .then_inc(yn_ready, 1)
                        a = t.plus(4)
                        if u == 4 and a.exists():
                            dve.wait_ge(tokens_out, a.total(1, 1))
                            for it in range(2):
                                nc.vector.bn_stats(st1[:, it, :], P_TOK[0:HALF, E * it:E * it + E])\
                                    .then_inc(stats_in, 1)
                            dve.wait_ge(stats_in, a.total(2, 2))
                            if a.after(1):
                                dve.wait_ge(qf_ready, a.total(2, 0))
                            settle(dve)
                            for it in range(2):
                                nc.vector.bn_aggr(mv1[:, it, :], st1[:, it, :]).then_inc(mv_ready, 1)
                        if u == 5 and a.exists():
                            s = a.place % 2
                            dve.wait_ge(rstd_ready, a.total(1, 1))
                            if a.after(2):
                                dve.wait_ge(v_ready, a.plus(-2).total(1, 1))
                            for it in range(2):
                                nc.vector.tensor_scalar(xn[s][:, it, :], P_TOK[0:HALF, E * it:E * it + E],
                                                        mv1[:, it, 0:1], rs1[:, it:it + 1], ALU.subtract,
                                                        ALU.mult).then_inc(xn_ready, 1)
                            if a.after(2):
                                dve.wait_ge(qst_ready, a.plus(-2).total(1, 1))
                            for it in range(2):
                                nc.vector.tensor_scalar(qf[s][:, it, :],
                                                        P_TOK[0:HALF, 256 + E * it:256 + E * it + E],
                                                        rs1[:, it:it + 1], None, ALU.mult).then_inc(qf_ready, 1)
                        a = t.plus(-1)
                        if u == 6 and a.exists():
                            dve.wait_ge(o_ready, a.total(1, 1))
                            nc.vector.bn_stats(ostats[:, bass.ds(a.index * 6, 6)],
                                               oT[:, bass.ds(a.index * TOK, TOK)]).then_inc(ostat_ready, 1)

                period_range(dve, period, 5, 1)

            @block.tensor
            def _(pe):
                pe.wait_ge(w_loaded, N_W)
                pe.wait_ge(pads_set, 3)
                pe.wait_ge(rows_ready, 1)
                for s in range(STEP):
                    i = nc.tensor.transpose(bank[s // 4][0:XROWS, E * (s % 4):E * (s % 4) + E],
                                            raw_rows[:, s, :, :].rearrange("e g k -> e (g k)"), ident[:, :])
                    if s % 4 == 3:
                        i.then_inc(setup_pe, 1)
                for k in range(HT):
                    i = nc.tensor.transpose(bank[2][:, 128 * k:128 * k + 128], raw_wo[:, 128 * k:128 * k + 128],
                                            ident[:, :])
                i.then_inc(setup_pe, 1)
                for k in range(HT):
                    i = nc.tensor.transpose(bank[3][:, 128 * k:128 * k + 128], raw_fc1[:, k, :], ident[:, :])
                i.then_inc(setup_pe, 1)
                for k in range(HT):
                    i = nc.tensor.transpose(bank[4][:, 64 * k:64 * k + 64], raw_fc2[:, 128 * k:128 * k + 128],
                                            ident[0:64, 0:64])
                i.then_inc(setup_pe, 1)
                nc.tensor.matmul(bank[5][:, 0:E], raw_wq.rearrange("p h c -> p (h c)"),
                                 raw_wk.rearrange("p h c -> p (h c)"), start=True, stop=True).then_inc(setup_pe, 1)
                pe.wait_ge(setup_dve, 3)
                for k in range(HT):
                    i = nc.tensor.matmul(bank[6][:, 0:E], wv_bd[:, k, :], woT[:, 128 * k:128 * k + 128],
                                         start=(k == 0), stop=(k == HT - 1))
                i.then_inc(setup_pe, 1)
                pe.wait_ge(setup_dve, 4)
                nc.tensor.matmul(bank[7][:, :], interp[:, :], w1T, start=True, stop=True).then_inc(setup_pe, 1)
                pe.wait_ge(setup_dve, 4 + 2 * HT + 2 + 1)
                nc.tensor.matmul(bank[5][:, 0:E], center[:, :], m_sb, start=True, stop=True).then_inc(setup_pe, 1)
                pe.wait_ge(setup_dve, 4 + 2 * HT + 2 + 1 + 3)
                pe.wait_ge(pads_set, 3 + 4 + RING + 2 + RING)

                def weigh(a, g):
                    grp, jt = g // 2, g % 2
                    pe.wait_ge(probs_ready, a.total(UNITS, 2 * g + 2))
                    if g == 0:
                        pe.wait_ge(v_ready, a.total(1, 1))
                        if a.after(1):
                            pe.wait_ge(y_ready, a.total(1, 0))
                    for hh in range(4):
                        i = nc.tensor.matmul(P_Y[32 * hh:32 * hh + 32, TOK * grp:TOK * grp + TOK],
                                             vpad[a.place][:, jt, 4 * grp + hh, :], probs[g % 2][:, hh, :],
                                             start=(jt == 0), stop=(jt == 1), skip_group_check=True)
                    i.then_inc(weighted, 1)

                def turn_stack(stack, pair2, done):
                    for q in range(2):
                        for it in range(2):
                            h = 2 * (2 * pair2 + q)
                            i = nc.tensor.transpose(P_MIX[:, TOK * q + HALF * it:TOK * q + HALF * it + HALF],
                                                    stack[:, it, h:h + 2, :].rearrange("p h c -> p (h c)"),
                                                    ident[0:HALF, 0:HALF])
                    i.then_inc(done, 1)

                def period(t):
                    for u in range(UNITS):
                        a = t.plus(2)
                        if a.exists():
                            it, e = u // PAIRS, u % 2
                            if u == 0:
                                pe.wait_ge(kT_ready, a.total(2, 2))
                                pe.wait_ge(qT_ready, a.total(2, 2))
                            if u >= 2 or a.after(1):
                                pe.wait_ge(max_taken, a.total(UNITS, u - 1))
                            for q in range(2):
                                pr = 2 * (u // 2 % 2) + q
                                i = nc.tensor.matmul(P_MAX[e][0:HALF, TOK * q:TOK * q + TOK],
                                                     qT[a.place][64 * e:64 * e + 64, pr, HALF * it:HALF * it + HALF],
                                                     kT[a.place][64 * e:64 * e + 64, pr, :], start=True, stop=True)
                            i.then_inc(max_scored, 1)
                        a = t.plus(-1)
                        if u == 0 and a.exists():
                            weigh(a, 3)
                        a = t.plus(1)
                        if u == 1 and a.exists():
                            pe.wait_ge(negm_ready, a.total(1, 1))
                            if a.plus(2).after(1) and a.plus(2).exists():
                                pe.wait_ge(qf_ready, a.plus(2).total(2, 2))
                            for it in range(2):
                                i = nc.tensor.transpose(P_TOK[0:HEADS, HALF * it:HALF * it + HALF], negm[:, it, :],
                                                        ident[0:HALF, 0:HALF])
                            i.then_inc(m_turned, 1)
                        a = t.plus(-1)
                        if u == 2 and a.exists():
                            pe.wait_ge(y_ready, a.total(1, 1))
                            if a.plus(2).exists():
                                pe.wait_ge(mT_ready, a.plus(2).total(1, 1))
                            for it in range(2):
                                for grp in range(2):
                                    n = 2 * it + grp
                                    i = nc.tensor.transpose(P_TOK[0:HALF, 128 * n:128 * n + 128],
                                                            ysb[:, grp, HALF * it:HALF * it + HALF], ident[:, :])
                            i.then_inc(y_turned, 1)
                        a = t.plus(3)
                        if u in (1, 2) and a.exists():
                            if u == 1:
                                pe.wait_ge(kst_ready, a.total(1, 1))
                                if a.after(1):
                                    pe.wait_ge(qT_ready, a.total(2, 0))
                            else:
                                pe.wait_ge(kT_ready, a.total(2, 1))
                            turn_stack(kst[a.place % 2], u - 1, k_turned)
                        if u == 3 and a.exists():
                            pe.wait_ge(qst_ready, a.total(1, 1))
                            pe.wait_ge(kT_ready, a.total(2, 2))
                            turn_stack(qst[a.place % 2], 0, q_turned)
                        a = t.plus(-1)
                        if u == 4 and a.exists():
                            pe.wait_ge(yn_ready, a.total(1, 1))
                            if a.plus(4).exists():
                                pe.wait_ge(qT_ready, a.plus(4).total(2, 1))
                            for it in range(2):
                                i = nc.tensor.transpose(P_MIX[:, HALF * it:HALF * it + HALF], yn[:, it, :],
                                                        ident[0:HALF, 0:HALF])
                            i.then_inc(yn_turned, 1)
                        if u == 5 and a.exists():
                            pe.wait_ge(ynT_ready, a.total(1, 1))
                            nc.tensor.matmul(P_MIX[:, 0:TOK], w_out[:, :], ynT[:, :], start=True, stop=True)\
                                .then_inc(projected, 1)
                        a = t.plus(3)
                        if u == 6 and a.exists():
                            if a.plus(-4).exists():
                                pe.wait_ge(o_ready, a.plus(-4).total(1, 1))
                            pe.wait_ge(qT_ready, a.total(2, 1))
                            turn_stack(qst[a.place % 2], 1, q_turned)
                        a = t.plus(4)
                        if u == 4 and a.exists():
                            pe.wait_ge(h_ready, a.total(1, 1))
                            if a.plus(-5).exists():
                                pe.wait_ge(yn_ready, a.plus(-5).total(1, 1))
                            if a.plus(-3).exists():
                                pe.wait_ge(mT_ready, a.plus(-3).total(1, 1))
                            for it in range(2):
                                nc.tensor.transpose(P_TOK[0:HALF, E * it:E * it + E],
                                                    hT[a.place][:, HALF * it:HALF * it + HALF], ident[:, :])
                                i = nc.tensor.matmul(P_TOK[0:HALF, 256 + E * it:256 + E * it + E],
                                                     hT[a.place][:, HALF * it:HALF * it + HALF], w_q[:, :],
                                                     start=True, stop=True)
                            i.then_inc(tokens_out, 1)
                        if t.exists():
                            jt, e = u // 2 % 2, u % 2
                            if u == 0:
                                pe.wait_ge(shift_put[t.place], t.turn(RING, 32))
                            if u >= 2 or t.after(1):
                                pe.wait_ge(probs_ready, t.total(UNITS, u - 1))
                            for q in range(2):
                                pr = 2 * (u // 4) + q
                                i = nc.tensor.matmul(P_SC[e][0:HALF, TOK * q:TOK * q + TOK],
                                                     kT[t.place][64 * e:64 * e + 64, pr, HALF * jt:HALF * jt + HALF],
                                                     qT[t.place][64 * e:64 * e + 64, pr, :], start=True, stop=True)
                            i.then_inc(scored, 1)
                            if u in (2, 4, 6):
                                weigh(t, u // 2 - 1)
                        a = t.plus(5)
                        if a.exists():
                            if u == 0:
                                pe.wait_ge(x_loaded[a.place % 2], a.turn(2, 16 * SPLIT * CH))
                                if a.after(1):
                                    pe.wait_ge(h_ready, a.total(1, 0))
                            i = nc.tensor.matmul(
                                P_EMB[:, 0:TOK].rearrange("p (y x) -> p y x", y=GRID), w_embed[:, u, :],
                                xin[a.place % 2][:, :, u:IMG - PATCH + u + 1:PATCH], start=(u == 0),
                                stop=(u == STEP - 1))
                            if u == STEP - 1:
                                i.then_inc(embedded, 1)

                period_range(pe, period, 5, 1)

        phase1.close()
        lifetime[0] = ctx
        UN = 2
        NP = B // 2
        yrel = [sb(f"yrel{k}", [E, 2, TOK]) for k in range(2)]
        hin = [sb(f"hin{k}", [E, 2, TOK]) for k in range(2)]
        x2 = [sb(f"x2{k}", [E, 2, TOK]) for k in range(2)]
        st2 = sb("st2", [HALF, 4, 6])
        mv2 = sb("mv2", [HALF, 4, 2])
        ve2 = sb("ve2", [HALF, 4])
        rs2 = sb("rs2", [HALF, 4])
        ln = [sb(f"ln{k}", [HALF, 4, E]) for k in range(2)]
        res = [sb(f"res{k}", [HALF, 4, E]) for k in range(2)]
        z = sb("z", [HALF, 2, E])
        zT = [sb(f"zT{k}", [E, 2 * HALF]) for k in range(2)]
        hid = [sb(f"hid{k}", [128, HT, 2 * HALF]) for k in range(2)]
        fin = [sb(f"fin{k}", [HALF, 4, E]) for k in range(2)]
        Q_T, Q_Z, Q_H, Q_D = bank[0:2], bank[2], bank[4:6], bank[6]

        h_back = [sem(f"h_back{k}") for k in range(2)]
        stored = [sem(f"stored{k}") for k in range(2)]
        rel_ready = sem("rel_ready")
        x2_ready = sem("x2_ready")
        x2_turned = sem("x2_turned")
        st2_in = sem("st2_in")
        mv2_ready = sem("mv2_ready")
        ve2_ready = sem("ve2_ready")
        rs2_ready = sem("rs2_ready")
        ln_ready = sem("ln_ready")
        res_ready = sem("res_ready")
        z_ready = sem("z_ready")
        z_turned = sem("z_turned")
        zT_ready = sem("zT_ready")
        hid_out = sem("hid_out")
        hid_ready = sem("hid_ready")
        ffn_out = sem("ffn_out")
        fin_ready = sem("fin_ready")

        class Pair(Image):

            def __init__(self, block, place):
                self.fixed = isinstance(block, int)
                self.block = block + place // UN
                self.place = place % UN
                self.index = self.block * UN + self.place

            def plus(self, d):
                return Pair(self.block, self.place + d)

            def exists(self, count=NP):
                return not self.fixed or 0 <= self.index < count

            def total(self, per, c):
                return self.block * (UN * per) + (self.place * per + c)

            def turn(self, slots, per):
                return self.block * (UN // slots * per) + (self.place // slots + 1) * per

        def pair_range(eng, period, lead):
            for t in range(-lead, UN):
                period(Pair(0, t))
            with eng.Fori(1, NP // UN - 2) as i:
                for k in range(UN):
                    period(Pair(i, k))
            for t in range(NP - 2 * UN, NP):
                period(Pair(0, t))

        h_pairs = h_dram.rearrange("b (q r) e t -> (b q) e r t", r=2)
        out_pairs = out.rearrange("(q r) (p d) e -> q p r (d e)", r=2, d=2)

        with nc.Block() as block:

            @block.sync
            def _(sp):
                def period(t):
                    a = t.plus(4)
                    if a.exists():
                        if a.after(2):
                            sp.wait_ge(x2_ready, a.plus(-2).total(1, 1))
                        settle(sp)
                        sp.dma_start(hin[a.place][:, :, :], h_pairs[a.index]).then_inc(h_back[a.place], 16)
                    if t.exists():
                        sp.wait_ge(fin_ready, t.total(1, 1))
                        settle(sp)
                        sp.dma_start(out_pairs[t.index],
                                     fin[t.place][:, :, :].rearrange("p (r d) e -> p r (d e)", r=2))\
                            .then_inc(stored[t.place], 16)

                pair_range(sp, period, 4)
                for k in range(UN):
                    sp.wait_ge(stored[k], 16 * (NP // UN))

            @block.vector
            def _(dve):
                nc.vector.bn_aggr(bn[:, 0:2], ostats[:, :]).then_inc(bn_ready, 1)
                dve.wait_ge(bn_ready, 3)
                nc.vector.tensor_tensor(bn[:, 3:4], bn[:, 2:3], gam[:, :], ALU.mult).then_inc(bn_ready, 1)
                dve.wait_ge(bn_ready, 4)
                nc.vector.tensor_tensor(bn[:, 4:5], bn[:, 0:1], bn[:, 3:4], ALU.mult).then_inc(bn_ready, 1)
                dve.wait_ge(bn_ready, 5)
                nc.vector.tensor_tensor(bn[:, 5:6], bet[:, :], bn[:, 4:5], ALU.subtract).then_inc(bn_ready, 1)

                def period(t):
                    a = t.plus(2)
                    if a.exists():
                        tiles = Q_T[a.place][0:HALF, :].rearrange("p (n e) -> p n e", n=4)
                        dve.wait_ge(x2_turned, a.total(1, 1))
                        for n in range(4):
                            nc.vector.bn_stats(st2[:, n, :], tiles[:, n, :]).then_inc(st2_in, 1)
                        dve.wait_ge(st2_in, a.total(4, 4))
                        if a.after(1):
                            dve.wait_ge(ln_ready, a.total(4, 0))
                        settle(dve)
                        for n in range(4):
                            nc.vector.bn_aggr(mv2[:, n, :], st2[:, n, :]).then_inc(mv2_ready, 1)
                    if t.exists():
                        dve.wait_ge(ffn_out, t.total(1, 1))
                        if t.after(2):
                            dve.wait_ge(stored[t.place], t.plus(-2).turn(UN, 16))
                        for r in range(2):
                            i = nc.vector.tensor_tensor(
                                fin[t.place][:, 2 * r:2 * r + 2, :], res[t.place][:, 2 * r:2 * r + 2, :],
                                Q_D[0:HALF, E * r:E * r + E].unsqueeze(1).to_broadcast([HALF, 2, E]), ALU.add)
                        i.then_inc(fin_ready, 1)
                    if a.exists():
                        dve.wait_ge(rs2_ready, a.total(1, 1))
                        if a.after(2):
                            dve.wait_ge(z_ready, a.plus(-2).total(1, 1))
                        for n in range(4):
                            nc.vector.tensor_scalar(ln[a.place][:, n, :], tiles[:, n, :], mv2[:, n, 0:1],
                                                    rs2[:, n:n + 1], ALU.subtract, ALU.mult).then_inc(ln_ready, 1)
                        dve.wait_ge(ln_ready, a.total(4, 4))
                        nc.vector.tensor_tensor(res[a.place][:, :, :], tiles, ln[a.place][:, :, :], ALU.add)\
                            .then_inc(res_ready, 1)

                pair_range(dve, period, 4)

            @block.gpsimd
            def _(pool):
                pool.wait_ge(bn_ready, 1)
                settle(pool)
                pool.tensor_scalar(bn[:, 4:5], bn[:, 1:2], EPS, None, ALU.add).then_inc(bn_ready, 1)
                pool.wait_ge(bn_ready, 2)
                pool.tensor_tensor(bn[:, 2:3], bn[:, 4:5], minus_half[:, 0:1], ALU.pow).then_inc(bn_ready, 1)

                def period(t):
                    a = t.plus(3)
                    if a.exists():
                        pool.wait_ge(rel_ready, a.total(1, 1))
                        pool.wait_ge(h_back[a.place], a.turn(UN, 16))
                        if a.after(2):
                            pool.wait_ge(x2_turned, a.plus(-2).total(1, 1))
                        pool.tensor_tensor(x2[a.place][:, :, :], yrel[a.place][:, :, :], hin[a.place][:, :, :],
                                           ALU.add).then_inc(x2_ready, 1)
                    a = t.plus(2)
                    if a.exists():
                        pool.wait_ge(mv2_ready, a.total(4, 4))
                        if a.after(1):
                            pool.wait_ge(ln_ready, a.total(4, 0))
                        settle(pool)
                        pool.tensor_scalar(ve2[:, :], mv2[:, :, 1], EPS, None, ALU.add).then_inc(ve2_ready, 1)
                        pool.wait_ge(ve2_ready, a.total(1, 1))
                        pool.tensor_tensor(rs2[:, :], ve2[:, :], minus_half[0:HALF, :], ALU.pow)\
                            .then_inc(rs2_ready, 1)
                        pool.wait_ge(ln_ready, a.total(4, 4))
                        if a.after(1):
                            pool.wait_ge(z_turned, a.total(1, 0))
                        pool.tensor_tensor(z[:, :, :], ln[a.place][:, 0::2, :], ln[a.place][:, 1::2, :],
                                           ALU.add).then_inc(z_ready, 1)

                pair_range(pool, period, 4)

            @block.scalar
            def _(act):
                act.wait_ge(bn_ready, 6)

                def period(t):
                    a = t.plus(4)
                    if a.exists():
                        if a.after(2):
                            act.wait_ge(x2_ready, a.plus(-2).total(1, 1))
                        nc.scalar.activation(yrel[a.place][:, :, :].rearrange("p r t -> p (r t)"),
                                             oT[:, bass.ds(a.index * (2 * TOK), 2 * TOK)], ACT.Relu,
                                             bias=bn[:, 5:6], scale=bn[:, 3:4]).then_inc(rel_ready, 1)
                    a = t.plus(1)
                    if a.exists():
                        act.wait_ge(z_turned, a.total(1, 1))
                        if a.after(2):
                            act.wait_ge(ffn_out, a.plus(-2).total(1, 1))
                        nc.scalar.activation(zT[a.place][:, :], Q_Z[:, 0:2 * HALF], ACT.Copy).then_inc(zT_ready, 1)
                        for k in range(HT):
                            act.wait_ge(hid_out, a.total(2, k // 2 + 1))
                            nc.scalar.activation(hid[a.place][:, k, :],
                                                 Q_H[k // 2][:, TOK * (k % 2):TOK * (k % 2) + TOK], ACT.Gelu,
                                                 bias=b_ffn1[:, k:k + 1]).then_inc(hid_ready, 1)

                pair_range(act, period, 4)

            @block.tensor
            def _(pe):
                def period(t):
                    a = t.plus(2)
                    if a.exists():
                        pe.wait_ge(x2_ready, a.total(1, 1))
                        if a.after(2):
                            pe.wait_ge(res_ready, a.plus(-2).total(1, 1))
                        for r in range(2):
                            for d in range(2):
                                n = 2 * r + d
                                i = nc.tensor.transpose(Q_T[a.place][0:HALF, E * n:E * n + E],
                                                        x2[a.place][:, r, d::2], ident[:, :])
                        i.then_inc(x2_turned, 1)
                    a = t.plus(1)
                    if a.exists():
                        pe.wait_ge(z_ready, a.total(1, 1))
                        if a.after(1):
                            pe.wait_ge(zT_ready, a.total(1, 0))
                        for r in range(2):
                            i = nc.tensor.transpose(Q_Z[:, HALF * r:HALF * r + HALF], z[:, r, :],
                                                    ident[0:HALF, 0:HALF])
                        i.then_inc(z_turned, 1)
                    if t.exists():
                        pe.wait_ge(hid_ready, t.total(HT, HT))
                        if t.after(1):
                            pe.wait_ge(fin_ready, t.total(1, 0))
                        for r in range(2):
                            o = Q_D[0:HALF, E * r:E * r + E]
                            for k in range(HT):
                                nc.tensor.matmul(o, hid[t.place][:, k, HALF * r:HALF * r + HALF], w_ffn2[:, k, :],
                                                 start=(k == 0), stop=False)
                            nc.tensor.matmul(o, zT[t.place][:, HALF * r:HALF * r + HALF], pairsum[:, :],
                                             start=False, stop=False)
                            i = nc.tensor.matmul(o, ones[:, :], b_ffn2[:, :], start=False, stop=True)
                        i.then_inc(ffn_out, 1)
                    if a.exists():
                        pe.wait_ge(zT_ready, a.total(1, 1))
                        for k in range(HT):
                            if k % 2 == 0 and a.after(1):
                                pe.wait_ge(hid_ready, a.total(HT, k + 2 - HT))
                            i = nc.tensor.matmul(Q_H[k // 2][:, TOK * (k % 2):TOK * (k % 2) + TOK],
                                                 w_ffn1[:, 128 * k:128 * k + 128], zT[a.place][:, :],
                                                 start=True, stop=True)
                            if k % 2:
                                i.then_inc(hid_out, 1)

                pair_range(pe, period, 4)


_INS = ['x', 'L0_tok_w', 'L0_tok_b', 'L0_attn_wq', 'L0_attn_wk', 'L0_attn_wv', 'L0_attn_wo', 'L0_attn_gamma',
        'L0_attn_beta', 'L0_ffn_fc1_w', 'L0_ffn_fc1_b', 'L0_ffn_fc2_w', 'L0_ffn_fc2_b']


def shape_constants():
    ident = np.eye(E, dtype=np.float32)
    center = (np.eye(E) - 1.0 / E).astype(np.float32)
    heads = np.kron(np.eye(HEADS), np.full((C, C), DH ** -0.5)).astype(np.float32)
    n, m = E // 2, E
    pos = np.linspace(0.0, 1.0, m, dtype=np.float32) * np.float32(n - 1)
    i0 = np.clip(np.floor(pos).astype(np.int64), 0, n - 2)
    w = pos - i0.astype(np.float32)
    interp = np.zeros((m, n), np.float32)
    interp[np.arange(m), i0] = 1 - w
    interp[np.arange(m), i0 + 1] = w
    interp = np.repeat(0.5 * interp, 2, axis=1)
    pair = np.kron(np.eye(n), np.full((2, 2), -0.25)).astype(np.float32)
    return {"c_ident": ident, "c_center": center, "c_heads": heads,
            "c_interp": np.ascontiguousarray(interp, np.float32), "c_pair": pair}


def kernel(**inputs):
    import concourse.bacc as _bacc
    from concourse.bass_utils import run_bass_kernel_spmd as _run

    nc = _bacc.Bacc("TRN2", target_bir_lowering=False, num_devices=1)
    arrays, args = {}, []
    for name, a in [(n, inputs[n]) for n in _INS] + list(shape_constants().items()):
        a = np.ascontiguousarray(a)
        arrays[f"in_{name}"] = a
        args.append(nc.dram_tensor(f"in_{name}", a.shape, mybir.dt.from_np(a.dtype), kind="ExternalInput").ap())
    out = nc.dram_tensor("out_0", (B, TOK, E), F32, kind="ExternalOutput").ap()
    vit_layer(nc, *args, out)
    r = _run(nc, [arrays], core_ids=[0])
    return r.results[0]["out_0"]
```

```python
import numpy as np
import concourse.bass as bass
from concourse import mybir
from contextlib import ExitStack


F32 = mybir.dt.float32
F32R = mybir.dt.float32r
ALU = mybir.AluOpType
ACT = mybir.ActivationFunctionType
AX = mybir.AxisListType

B, CH, IMG, PATCH = 128, 3, 224, 16
GRID = IMG // PATCH
TOK = GRID * GRID
HALF = TOK // 2
E = 128
HEADS, DH = 8, 64
C = E // HEADS
PAIRS = HEADS // 2
SPLIT = 2
STEP = PATCH // SPLIT
XROWS = SPLIT * CH * PATCH
HID = 512
HT = HID // 128
EPS = 1e-5
RING = 4
UNITS = 8
WARM_UPS = 14
AUG = 2 * C


class Image:

    def __init__(self, block, place):
        self.fixed = isinstance(block, int)
        self.block = block + place // RING
        self.place = place % RING
        self.index = self.block * RING + self.place

    def plus(self, d):
        return Image(self.block, self.place + d)

    def exists(self, count=B):
        return not self.fixed or 0 <= self.index < count

    def after(self, d):
        return not self.fixed or self.index >= d

    def total(self, per, c):
        return self.block * (RING * per) + (self.place * per + c)

    def turn(self, slots, per):
        return self.block * (RING // slots * per) + (self.place // slots + 1) * per


def vit_layer(nc, x, tok_w, tok_b, wq, wk, wv, wo, gamma, beta, fc1_w, fc1_b, fc2_w, fc2_b,
              c_ident, c_center, c_heads, c_interp, c_pair, out):
    ctx = ExitStack()
    with ctx:
        lifetime = [ctx]

        def sb(name, shape, dt=F32):
            return lifetime[0].enter_context(nc.sbuf_tensor(name, shape, dt))

        def sem(name):
            return ctx.enter_context(nc.semaphore(name))

        ctx.enter_context(nc.allow_non_contiguous_dma("short rows of small weights"))
        h_dram = nc.dram_tensor("h_spill", [B // RING, RING, E, TOK], F32, kind="Internal").ap()

        ident = sb("ident", [128, 128])
        identr = sb("identr", [128, 128], F32R)
        pairsum = sb("pairsum", [E, E])
        w_embed = sb("w_embed", [XROWS, STEP, E])
        b_embed = sb("b_embed", [E, 1])
        w_q = sb("w_q", [E, E])
        w_out = sb("w_out", [E, E])
        w_ffn1 = sb("w_ffn1", [E, HID])
        w_ffn2 = sb("w_ffn2", [128, HT, E])
        b_ffn1 = sb("b_ffn1", [128, HT])
        b_ffn2 = sb("b_ffn2", [E, 1])
        gam = sb("gam", [E, 1])
        bet = sb("bet", [E, 1])
        oT = sb("oT", [E, B * TOK])
        ostats = sb("ostats", [E, B * 6])
        bn = sb("bn", [E, 6])

        minus_half = sb("minus_half", [128, 4])

        phase1 = ctx.enter_context(ExitStack())
        lifetime[0] = phase1
        xin = [sb(f"xin{k}", [XROWS, GRID, IMG]) for k in range(2)]
        hT = [sb(f"hT{k}", [E, TOK]) for k in range(2)]
        st1 = sb("st1", [HALF, 2, 6])
        mv1 = sb("mv1", [HALF, 2, 2])
        ve1 = sb("ve1", [HALF, 2])
        rs1 = sb("rs1", [HALF, 2])
        xn = [sb(f"xn{k}", [HALF, 2, E]) for k in range(2)]
        qf = [sb(f"qf{k}", [HALF, 2, E]) for k in range(2)]
        kst = [sb(f"kst{k}", [HALF, 2, HEADS, 4 * C]) for k in range(2)]
        qst = [sb(f"qst{k}", [HALF, 2, HEADS, 4 * C]) for k in range(2)]
        vpad = [sb(f"vpad{k}", [HALF, 2, HEADS, 2 * C]) for k in range(RING)]
        kT = [sb(f"kT{k}", [128, PAIRS, TOK], F32R) for k in range(RING)]
        qT = [sb(f"qT{k}", [128, PAIRS, TOK], F32R) for k in range(RING)]
        rmax = [sb(f"rmax{k}", [HALF, 2, HEADS]) for k in range(2)]
        negm = sb("negm", [HALF, 2, HEADS])
        mT = [sb(f"mT{k}", [HEADS, TOK], F32R) for k in range(2)]
        probs = [sb(f"probs{k}", [HALF, 4, TOK]) for k in range(2)]
        ysb = sb("ysb", [128, 2, TOK])
        rden = sb("rden", [HALF, 4 * 4])
        yn = sb("yn", [HALF, 2, E])
        ynT = sb("ynT", [E, TOK])

        bank = [ctx.enter_context(nc.psum_tensor(f"bank{k}", [128, 512], F32)) for k in range(8)]
        P_EMB, P_TOK, P_MIX, P_Y = bank[0], bank[1], bank[2], bank[3]
        P_MAX, P_SC = bank[4:6], bank[6:8]

        settled = sem("settled")
        tok_loaded = sem("tok_loaded")
        w_loaded = sem("w_loaded")
        pads_set = sem("pads_set")
        rows_ready = sem("rows_ready")
        setup_pe = sem("setup_pe")
        setup_dve = sem("setup_dve")
        x_loaded = [sem(f"x_loaded{k}") for k in range(2)]
        h_spilled = [sem(f"h_spilled{k}") for k in range(RING)]
        shift_put = [sem(f"shift_put{k}") for k in range(RING)]
        embedded = sem("embedded")
        h_ready = sem("h_ready")
        tokens_out = sem("tokens_out")
        stats_in = sem("stats_in")
        mv_ready = sem("mv_ready")
        ve1_ready = sem("ve1_ready")
        rstd_ready = sem("rstd_ready")
        xn_ready = sem("xn_ready")
        qf_ready = sem("qf_ready")
        khi_ready = sem("khi_ready")
        kst_ready = sem("kst_ready")
        qhi_ready = sem("qhi_ready")
        qst_ready = sem("qst_ready")
        v_ready = sem("v_ready")
        k_turned = sem("k_turned")
        q_turned = sem("q_turned")
        kT_ready = sem("kT_ready")
        qT_ready = sem("qT_ready")
        max_scored = sem("max_scored")
        max_taken = sem("max_taken")
        negm_ready = sem("negm_ready")
        m_turned = sem("m_turned")
        mT_ready = sem("mT_ready")
        scored = sem("scored")
        probs_ready = sem("probs_ready")
        weighted = sem("weighted")
        y_ready = sem("y_ready")
        y_turned = sem("y_turned")
        rden_ready = sem("rden_ready")
        yn_ready = sem("yn_ready")
        yn_turned = sem("yn_turned")
        ynT_ready = sem("ynT_ready")
        projected = sem("projected")
        o_ready = sem("o_ready")
        ostat_ready = sem("ostat_ready")
        bn_ready = sem("bn_ready")

        raw = oT[:, 0:768]
        raw_wo = oT[:, 768:1280]
        raw_fc1 = oT[:, 1280:1792].rearrange("p (k m) -> p k m", k=HT)
        raw_fc2 = oT[0:E // 2, 1792:2304]
        raw_wq = oT[0:DH, 2304:2432].rearrange("p (h c) -> p h c", h=HEADS)
        raw_wk = oT[0:DH, 2432:2560].rearrange("p (h c) -> p h c", h=HEADS)
        wv_bd = oT[:, 2560:3072].rearrange("p (t c) -> p t c", t=HT)
        wv_diag = oT[:, 2560:3200].rearrange("p (t w) -> p t w", w=128 + 2 * C)
        woT = oT[:, 3072:3584]
        w1T = oT[:, 3584:4096]
        m_sb = oT[:, 4096:4224]
        raw_rows = oT[:, 4224:4992].rearrange("e (s g k) -> e s g k", s=STEP, g=SPLIT)
        center = oT[:, 4992:5120]
        headmask = oT[:, 5120:5248]
        interp = oT[:, 5248:5376]
        b_ffn2_raw = oT[:, 5376:5377]
        N_W = 16 * 17

        xv = x.rearrange("b c (hp py) w -> b c py hp w", py=PATCH)

        def settle(eng):
            eng.sem_inc(settled, 1)

        def period_range(eng, period, lead, tail):
            for t in range(-lead, RING):
                period(Image(0, t))
            with eng.Fori(1, B // RING - 2) as i:
                for k in range(RING):
                    period(Image(i, k))
            for t in range(B - 2 * RING, B + tail):
                period(Image(0, t))

        block1 = nc.Block()
        with block1 as block:

            @block.sync
            def _(sp):
                sp.dma_start(ident[:, :], c_ident).then_inc(tok_loaded, 16)
                sp.dma_start(raw, tok_w).then_inc(tok_loaded, 16)
                for dst, src in ((center, c_center), (headmask, c_heads), (interp, c_interp), (pairsum, c_pair)):
                    sp.dma_start(dst[:, :], src).then_inc(w_loaded, 16)
                for dst, src in ((b_embed, tok_b), (gam, gamma), (bet, beta)):
                    sp.dma_start(dst[:, :], src.rearrange("(p a) -> p a", a=1)).then_inc(w_loaded, 16)
                sp.dma_start(raw_wq, wq.rearrange("h e c -> e h c")).then_inc(w_loaded, 16)
                sp.dma_start(raw_wk, wk.rearrange("h e c -> e h c")).then_inc(w_loaded, 16)
                sp.dma_start(raw_wo, wo).then_inc(w_loaded, 16)
                sp.dma_start(raw_fc1, fc1_w.rearrange("(k p) m -> p k m", p=128)).then_inc(w_loaded, 16)
                sp.dma_start(raw_fc2, fc2_w).then_inc(w_loaded, 16)
                sp.dma_start(b_ffn1[:, :], fc1_b.rearrange("(k p) -> p k", p=128)).then_inc(w_loaded, 16)
                for d in range(2):
                    sp.dma_start(b_ffn2_raw[d::2, :], fc2_b.rearrange("(p a) -> p a", a=1)).then_inc(w_loaded, 16)
                sp.wait_ge(pads_set, 1)
                for d in range(2):
                    sp.dma_start(wv_diag[DH * d:DH * d + DH, :, C * d:C * d + C],
                                 wv[d::2, :, :].rearrange("t e c -> e t c")).then_inc(w_loaded, 16)

                def load(img):
                    k = img.place % 2
                    if img.after(2):
                        sp.wait_ge(embedded, img.plus(-2).total(1, 1))
                    settle(sp)
                    for g in range(SPLIT):
                        for c in range(CH):
                            p, n = (g * CH + c) * PATCH, IMG - g * STEP
                            sp.dma_start(xin[k][p:p + PATCH, :, 0:n],
                                         xv[img.index, c, :, :, g * STEP:IMG]).then_inc(x_loaded[k], 16)

                def period(t):
                    a = t.plus(4)
                    if a.exists():
                        sp.wait_ge(h_ready, a.total(1, 1))
                        settle(sp)
                        sp.dma_start(h_dram[a.block, a.place], hT[a.place % 2][:, :]).then_inc(h_spilled[a.place], 16)
                    a = t.plus(1)
                    if a.exists():
                        sp.wait_ge(mT_ready, a.total(1, 1))
                        settle(sp)
                        for e in range(2):
                            sp.dma_start(qT[a.place][64 * e + AUG:64 * e + AUG + 1, :, :].bitcast(F32),
                                         mT[a.place % 2][PAIRS * e:PAIRS * e + PAIRS, :].bitcast(F32))\
                              .then_inc(shift_put[a.place], 16)
                    a = t.plus(7)
                    if a.exists():
                        load(a)

                period_range(sp, period, 7, 0)
                for k in range(RING):
                    sp.wait_ge(h_spilled[k], 16 * (B // RING))

            @block.gpsimd
            def _(pool):
                pool.memset(wv_bd[:, :, :], 0.0).then_inc(pads_set, 1)
                pool.memset(minus_half[:, :], -0.5).then_inc(pads_set, 1)
                for k in range(2):
                    pool.memset(kst[k][:, :, :, :], 0.0).then_inc(pads_set, 1)
                    pool.memset(qst[k][:, :, :, :], 0.0).then_inc(pads_set, 1)
                for k in range(RING):
                    pool.memset(vpad[k][:, :, :, :], 0.0).then_inc(pads_set, 1)
                pool.wait_ge(pads_set, 2 + 4 + RING)
                for k in range(2):
                    pool.memset(kst[k][:, :, :, AUG:AUG + 1], 1.0).then_inc(pads_set, 1)
                for k in range(RING):
                    pool.memset(vpad[k][:, :, :, C:C + 1], 1.0).then_inc(pads_set, 1)
                pool.wait_ge(pads_set, 2 + 4 + RING + 2 + RING)

                def period(t):
                    a = t.plus(1)
                    if a.exists():
                        pool.wait_ge(max_taken, a.total(UNITS, UNITS))
                        if a.after(1):
                            pool.wait_ge(m_turned, a.total(1, 0))
                        settle(pool)
                        pool.tensor_scalar(negm[:, :, :].bitcast(F32R), rmax[a.place % 2][:, :, :], -1.0,
                                           None, ALU.mult).then_inc(negm_ready, 1)
                    a = t.plus(3)
                    if a.exists():
                        pool.wait_ge(qhi_ready, a.total(1, 1))
                        pool.tensor_tensor(qst[a.place % 2][:, :, :, C:2 * C].bitcast(F32R),
                                           qf[a.place % 2][:, :, :].rearrange("p t (h c) -> p t h c", c=C),
                                           qst[a.place % 2][:, :, :, 0:C], ALU.subtract).then_inc(qst_ready, 1)
                        pool.wait_ge(xn_ready, a.total(2, 2))
                        if a.after(4):
                            pool.wait_ge(weighted, a.plus(-4).total(4, 4))
                        settle(pool)
                        pool.tensor_scalar(vpad[a.place][:, :, :, 0:C],
                                           xn[a.place % 2][:, :, :].rearrange("p t (h c) -> p t h c", c=C),
                                           1.0, None, ALU.mult).then_inc(v_ready, 1)
                    a = t.plus(4)
                    if a.exists():
                        s = a.place % 2
                        pool.wait_ge(mv_ready, a.total(2, 2))
                        if a.after(1):
                            pool.wait_ge(qf_ready, a.total(2, 0))
                        settle(pool)
                        pool.tensor_scalar(ve1[:, :], mv1[:, :, 1], EPS, None, ALU.add).then_inc(ve1_ready, 1)
                        pool.wait_ge(ve1_ready, a.total(1, 1))
                        pool.tensor_tensor(rs1[:, :], ve1[:, :], minus_half[0:HALF, 0:2], ALU.pow)\
                            .then_inc(rstd_ready, 1)
                        pool.wait_ge(khi_ready, a.total(1, 1))
                        pool.tensor_tensor(kst[s][:, :, :, 3 * C:4 * C].bitcast(F32R),
                                           xn[s][:, :, :].rearrange("p t (h c) -> p t h c", c=C),
                                           kst[s][:, :, :, 0:C], ALU.subtract).then_inc(kst_ready, 1)

                period_range(pool, period, 7, 0)

            @block.scalar
            def _(act):
                act.wait_ge(w_loaded, N_W)

                def hi_parts(a, tokens, tokens_ready, stack, turned_out, step, done):
                    act.wait_ge(tokens_ready, a.total(2, 2))
                    if a.after(2):
                        act.wait_ge(turned_out, a.plus(-2).total(2, 2))
                    nc.scalar.activation(
                        stack[:, :, :, :].rearrange("p t h (b c) -> p (t h) b c", c=C)
                        [:, :, 0:step + 1:step, :].bitcast(F32R),
                        tokens[:, :, :].rearrange("p t (h c) -> p (t h) c", c=C).unsqueeze(2)
                        .to_broadcast([HALF, 2 * HEADS, 2, C]), ACT.Copy).then_inc(done, 1)

                def period(t):
                    for u in range(UNITS):
                        a = t.plus(4)
                        if u == 0 and a.exists():
                            act.wait_ge(embedded, a.total(1, 1))
                            if a.after(2):
                                b = a.plus(-2)
                                act.wait_ge(h_spilled[b.place], b.turn(RING, 16))
                                act.wait_ge(tokens_out, b.total(1, 1))
                            nc.scalar.activation(hT[a.place % 2][:, :], P_EMB[:, 0:TOK], ACT.Identity,
                                                 bias=b_embed[:, 0:1]).then_inc(h_ready, 1)
                        a = t.plus(-1)
                        if u == 1 and a.exists():
                            act.wait_ge(weighted, a.total(4, 4))
                            if a.after(1):
                                act.wait_ge(y_turned, a.total(1, 0))
                            nc.scalar.activation(ysb[:, :, :], P_Y[:, 0:2 * TOK], ACT.Copy).then_inc(y_ready, 1)
                        a = t.plus(3)
                        if u in (1, 2) and a.exists():
                            act.wait_ge(k_turned, a.total(2, u))
                            nc.scalar.activation(kT[a.place][:, 2 * u - 2:2 * u, :], P_MIX[:, 0:2 * TOK],
                                                 ACT.Copy).then_inc(kT_ready, 1)
                        if u in (3, 6) and a.exists():
                            v = u // 3 - 1
                            act.wait_ge(q_turned, a.total(2, v + 1))
                            nc.scalar.activation(qT[a.place][:, 2 * v:2 * v + 2, :], P_MIX[:, 0:2 * TOK],
                                                 ACT.Copy).then_inc(qT_ready, 1)
                        a = t.plus(-1)
                        if u == 4 and a.exists():
                            act.wait_ge(yn_turned, a.total(1, 1))
                            nc.scalar.activation(ynT[:, :], P_MIX[:, 0:TOK], ACT.Copy).then_inc(ynT_ready, 1)
                        if u == 5 and a.exists():
                            act.wait_ge(projected, a.total(1, 1))
                            nc.scalar.activation(oT[:, bass.ds(a.index * TOK, TOK)], P_MIX[:, 0:TOK],
                                                 ACT.Copy).then_inc(o_ready, 1)
                        if t.exists():
                            act.wait_ge(scored, t.total(UNITS, u + 1))
                            if u % 2 == 0 and (u >= 4 or t.after(1)):
                                act.wait_ge(weighted, t.total(4, u // 2 - 1))
                            e = 1 - u % 2
                            nc.scalar.activation(probs[u // 2 % 2][:, e::2, :],
                                                 P_SC[e][0:HALF, 0:2 * TOK], ACT.Exp)\
                                .then_inc(probs_ready, 1)
                        a = t.plus(4)
                        if u == 6 and a.exists():
                            hi_parts(a, xn[a.place % 2], xn_ready, kst[a.place % 2], k_turned, 1, khi_ready)
                        a = t.plus(3)
                        if u == 0 and a.exists():
                            hi_parts(a, qf[a.place % 2], qf_ready, qst[a.place % 2], q_turned, 3, qhi_ready)

                period_range(act, period, 5, 1)

            @block.vector
            def _(dve):
                def turned(v, dst, src):
                    dve.wait_ge(setup_pe, v)
                    nc.vector.tensor_copy(dst, src).then_inc(setup_dve, 1)

                dve.wait_ge(tok_loaded, 32)
                dve.wait_ge(pads_set, 2)
                nc.vector.tensor_copy(identr[:, :], ident[:, :]).then_inc(rows_ready, 1)
                nc.vector.tensor_copy(raw_rows, raw.rearrange("e (cp g s) -> e s g cp", g=SPLIT, s=STEP))\
                    .then_inc(rows_ready, 1)
                for g in range(2):
                    turned(g + 1, w_embed[:, 4 * g:4 * g + 4, :], bank[g][0:XROWS, :])
                dve.wait_ge(w_loaded, N_W)
                turned(3, woT, bank[2][:, :])
                turned(4, w1T, bank[3][:, :])
                dve.wait_ge(setup_pe, 5)
                for k in range(HT):
                    for d in range(2):
                        nc.vector.tensor_scalar(w_ffn2[:, k, d::2], bank[4][:, 64 * k:64 * k + 64], 0.5, None,
                                                ALU.mult).then_inc(setup_dve, 1)
                nc.vector.tensor_scalar(b_ffn2[:, :], b_ffn2_raw[:, :], 0.5, None, ALU.mult).then_inc(setup_dve, 1)
                dve.wait_ge(setup_pe, 6)
                nc.vector.tensor_tensor(m_sb, bank[5][:, 0:E], headmask[:, :], ALU.mult).then_inc(setup_dve, 1)
                turned(7, w_out[:, :], bank[6][:, 0:E])
                turned(8, w_ffn1[:, :], bank[7][:, :])
                turned(9, w_q[:, :], bank[5][:, 0:E])

                def period(t):
                    for u in range(UNITS):
                        a = t.plus(2)
                        if a.exists():
                            dve.wait_ge(max_scored, a.total(UNITS, u + 1))
                            if u == 0 and a.after(2):
                                dve.wait_ge(negm_ready, a.plus(-2).total(1, 1))
                            it, first = u // PAIRS, PAIRS * (u % 2) + 2 * (u // 2 % 2)
                            nc.vector.reduce_max(
                                rmax[a.place % 2][:, it, first:first + 2],
                                P_MAX[u % 2][0:HALF, 0:2 * TOK].rearrange("p (q j) -> p q j", q=2), AX.X)\
                                .then_inc(max_taken, 1)
                        a = t.plus(1)
                        if u == 1 and a.exists():
                            dve.wait_ge(m_turned, a.total(1, 1))
                            if a.after(2):
                                dve.wait_ge(shift_put[(a.place + 2) % RING], a.plus(-2).turn(RING, 32))
                            nc.vector.tensor_copy(mT[a.place % 2][:, :], P_TOK[0:HEADS, 0:TOK])\
                                .then_inc(mT_ready, 1)
                        a = t.plus(-1)
                        if u == 2 and a.exists():
                            groups = P_TOK[0:HALF, :].rearrange("p (n c) -> p n c", c=2 * C)
                            dve.wait_ge(y_turned, a.total(1, 1))
                            nc.vector.reciprocal(rden[:, :], groups[:, :, C]).then_inc(rden_ready, 1)
                            dve.wait_ge(rden_ready, a.total(1, 1))
                            if a.after(1):
                                dve.wait_ge(yn_turned, a.total(1, 0))
                            nc.vector.tensor_tensor(
                                yn[:, :, :].rearrange("p t (h c) -> p (t h) c", c=C), groups[:, :, 0:C],
                                rden[:, :].unsqueeze(2).to_broadcast([HALF, 16, C]), ALU.mult)\
                                .then_inc(yn_ready, 1)
                        a = t.plus(4)
                        if u == 4 and a.exists():
                            dve.wait_ge(tokens_out, a.total(1, 1))
                            for it in range(2):
                                nc.vector.bn_stats(st1[:, it, :], P_TOK[0:HALF, E * it:E * it + E])\
                                    .then_inc(stats_in, 1)
                            dve.wait_ge(stats_in, a.total(2, 2))
                            if a.after(1):
                                dve.wait_ge(qf_ready, a.total(2, 0))
                            settle(dve)
                            for it in range(2):
                                nc.vector.bn_aggr(mv1[:, it, :], st1[:, it, :]).then_inc(mv_ready, 1)
                        if u == 5 and a.exists():
                            s = a.place % 2
                            dve.wait_ge(rstd_ready, a.total(1, 1))
                            if a.after(2):
                                dve.wait_ge(v_ready, a.plus(-2).total(1, 1))
                            for it in range(2):
                                nc.vector.tensor_scalar(xn[s][:, it, :], P_TOK[0:HALF, E * it:E * it + E],
                                                        mv1[:, it, 0:1], rs1[:, it:it + 1], ALU.subtract,
                                                        ALU.mult).then_inc(xn_ready, 1)
                            if a.after(2):
                                dve.wait_ge(qst_ready, a.plus(-2).total(1, 1))
                            for it in range(2):
                                nc.vector.tensor_scalar(qf[s][:, it, :],
                                                        P_TOK[0:HALF, 256 + E * it:256 + E * it + E],
                                                        rs1[:, it:it + 1], None, ALU.mult).then_inc(qf_ready, 1)
                        a = t.plus(-1)
                        if u == 6 and a.exists():
                            dve.wait_ge(o_ready, a.total(1, 1))
                            nc.vector.bn_stats(ostats[:, bass.ds(a.index * 6, 6)],
                                               oT[:, bass.ds(a.index * TOK, TOK)]).then_inc(ostat_ready, 1)

                period_range(dve, period, 5, 1)

            @block.tensor
            def _(pe):
                pe.wait_ge(tok_loaded, 32)
                pe.wait_ge(pads_set, 2)
                pe.wait_ge(rows_ready, 2)
                for s in range(STEP):
                    i = nc.tensor.transpose(bank[s // 4][0:XROWS, E * (s % 4):E * (s % 4) + E],
                                            raw_rows[:, s, :, :].rearrange("e g k -> e (g k)"), ident[:, :])
                    if s % 4 == 3:
                        i.then_inc(setup_pe, 1)
                pe.wait_ge(w_loaded, N_W)
                for k in range(HT):
                    i = nc.tensor.transpose(bank[2][:, 128 * k:128 * k + 128], raw_wo[:, 128 * k:128 * k + 128],
                                            ident[:, :])
                i.then_inc(setup_pe, 1)
                for k in range(HT):
                    i = nc.tensor.transpose(bank[3][:, 128 * k:128 * k + 128], raw_fc1[:, k, :], ident[:, :])
                i.then_inc(setup_pe, 1)
                for k in range(HT):
                    i = nc.tensor.transpose(bank[4][:, 64 * k:64 * k + 64], raw_fc2[:, 128 * k:128 * k + 128],
                                            ident[0:64, 0:64])
                i.then_inc(setup_pe, 1)
                nc.tensor.matmul(bank[5][:, 0:E], raw_wq.rearrange("p h c -> p (h c)"),
                                 raw_wk.rearrange("p h c -> p (h c)"), start=True, stop=True).then_inc(setup_pe, 1)
                pe.wait_ge(setup_dve, 3)
                for k in range(HT):
                    i = nc.tensor.matmul(bank[6][:, 0:E], wv_bd[:, k, :], woT[:, 128 * k:128 * k + 128],
                                         start=(k == 0), stop=(k == HT - 1))
                i.then_inc(setup_pe, 1)
                pe.wait_ge(setup_dve, 4)
                nc.tensor.matmul(bank[7][:, :], interp[:, :], w1T, start=True, stop=True).then_inc(setup_pe, 1)
                pe.wait_ge(setup_dve, 4 + 2 * HT + 1 + 1)
                nc.tensor.matmul(bank[5][:, 0:E], center[:, :], m_sb, start=True, stop=True).then_inc(setup_pe, 1)
                pe.wait_ge(setup_dve, 4 + 2 * HT + 1 + 1 + 3)
                pe.wait_ge(pads_set, 2 + 4 + RING + 2 + RING)

                def warm_up(a):
                    for k in range(WARM_UPS):
                        nc.tensor.matmul(P_Y[:, 0:2 * TOK], identr[:, :], kT[a.place][:, 0:2, :],
                                         start=True, stop=True)

                def weigh(a, g):
                    grp, jt = g // 2, g % 2
                    pe.wait_ge(probs_ready, a.total(UNITS, 2 * g + 2))
                    if g == 0:
                        pe.wait_ge(v_ready, a.total(1, 1))
                        if a.after(1):
                            pe.wait_ge(y_ready, a.total(1, 0))
                    for hh in range(4):
                        i = nc.tensor.matmul(P_Y[32 * hh:32 * hh + 32, TOK * grp:TOK * grp + TOK],
                                             vpad[a.place][:, jt, 4 * grp + hh, :], probs[g % 2][:, hh, :],
                                             start=(jt == 0), stop=(jt == 1), skip_group_check=True)
                    i.then_inc(weighted, 1)

                def turn_stack(stack, pair2, done):
                    for q in range(2):
                        for it in range(2):
                            h = 2 * (2 * pair2 + q)
                            i = nc.tensor.transpose(
                                P_MIX[:, TOK * q + HALF * it:TOK * q + HALF * it + HALF].bitcast(F32R),
                                stack[:, it, h:h + 2, :].rearrange("p h c -> p (h c)").bitcast(F32R),
                                identr[0:HALF, 0:HALF])
                    i.then_inc(done, 1)

                def period(t):
                    for u in range(UNITS):
                        a = t.plus(2)
                        if a.exists():
                            if u == 0:
                                pe.wait_ge(kT_ready, a.total(2, 2))
                                pe.wait_ge(qT_ready, a.total(2, 2))
                            if u >= 2 or a.after(1):
                                pe.wait_ge(max_taken, a.total(UNITS, u - 1))
                        for q in range(2):
                            if a.exists():
                                it, e, pr = u // PAIRS, u % 2, 2 * (u // 2 % 2) + q
                                i = nc.tensor.matmul(P_MAX[e][0:HALF, TOK * q:TOK * q + TOK],
                                                     qT[a.place][64 * e:64 * e + 64, pr, HALF * it:HALF * it + HALF],
                                                     kT[a.place][64 * e:64 * e + 64, pr, :], start=True, stop=True)
                                if q == 1:
                                    i.then_inc(max_scored, 1)
                            if t.exists():
                                jt, e, pr = u // 2 % 2, 1 - u % 2, 2 * (u // 4) + q
                                if q == 0 and u == 0:
                                    pe.wait_ge(shift_put[t.place], t.turn(RING, 32))
                                if q == 0 and (u >= 2 or t.after(1)):
                                    pe.wait_ge(probs_ready, t.total(UNITS, u - 1))
                                i = nc.tensor.matmul(P_SC[e][0:HALF, TOK * q:TOK * q + TOK],
                                                     kT[t.place][64 * e:64 * e + 64, pr, HALF * jt:HALF * jt + HALF],
                                                     qT[t.place][64 * e:64 * e + 64, pr, :], start=True, stop=True)
                                if q == 1:
                                    i.then_inc(scored, 1)
                        a = t.plus(-1)
                        if u == 2 and a.exists():
                            pe.wait_ge(y_ready, a.total(1, 1))
                            if a.plus(2).exists():
                                pe.wait_ge(mT_ready, a.plus(2).total(1, 1))
                            for it in range(2):
                                for grp in range(2):
                                    n = 2 * it + grp
                                    i = nc.tensor.transpose(P_TOK[0:HALF, 128 * n:128 * n + 128],
                                                            ysb[:, grp, HALF * it:HALF * it + HALF], ident[:, :])
                            i.then_inc(y_turned, 1)
                        a = t.plus(3)
                        if u in (1, 2) and a.exists():
                            if u == 1:
                                pe.wait_ge(kst_ready, a.total(1, 1))
                                if a.after(1):
                                    pe.wait_ge(qT_ready, a.total(2, 0))
                            else:
                                pe.wait_ge(kT_ready, a.total(2, 1))
                            turn_stack(kst[a.place % 2], u - 1, k_turned)
                        if u == 3 and a.exists():
                            pe.wait_ge(qst_ready, a.total(1, 1))
                            pe.wait_ge(kT_ready, a.total(2, 2))
                            turn_stack(qst[a.place % 2], 0, q_turned)
                        a = t.plus(-1)
                        if u == 4 and a.exists():
                            pe.wait_ge(yn_ready, a.total(1, 1))
                            if a.plus(4).exists():
                                pe.wait_ge(qT_ready, a.plus(4).total(2, 1))
                            for it in range(2):
                                i = nc.tensor.transpose(P_MIX[:, HALF * it:HALF * it + HALF], yn[:, it, :],
                                                        ident[0:HALF, 0:HALF])
                            i.then_inc(yn_turned, 1)
                        if u == 5 and a.exists():
                            pe.wait_ge(ynT_ready, a.total(1, 1))
                            nc.tensor.matmul(P_MIX[:, 0:TOK], w_out[:, :], ynT[:, :], start=True, stop=True)\
                                .then_inc(projected, 1)
                        a = t.plus(3)
                        if u == 6 and a.exists():
                            if a.plus(-4).exists():
                                pe.wait_ge(o_ready, a.plus(-4).total(1, 1))
                            pe.wait_ge(qT_ready, a.total(2, 1))
                            turn_stack(qst[a.place % 2], 1, q_turned)
                        a = t.plus(4)
                        if u == 4 and a.exists():
                            pe.wait_ge(h_ready, a.total(1, 1))
                            if a.plus(-5).exists():
                                pe.wait_ge(yn_ready, a.plus(-5).total(1, 1))
                            if a.plus(-3).exists():
                                pe.wait_ge(mT_ready, a.plus(-3).total(1, 1))
                            for it in range(2):
                                nc.tensor.transpose(P_TOK[0:HALF, E * it:E * it + E],
                                                    hT[a.place % 2][:, HALF * it:HALF * it + HALF], ident[:, :])
                                i = nc.tensor.matmul(P_TOK[0:HALF, 256 + E * it:256 + E * it + E],
                                                     hT[a.place % 2][:, HALF * it:HALF * it + HALF], w_q[:, :],
                                                     start=True, stop=True)
                            i.then_inc(tokens_out, 1)
                        if u == 2 and t.fixed and t.index == 0:
                            warm_up(t)
                        if u in (2, 4, 6) and t.exists():
                            weigh(t, u // 2 - 1)
                        a = t.plus(-1)
                        if u == 0 and a.exists():
                            weigh(a, 3)
                        a = t.plus(1)
                        if u == 1 and a.exists():
                            pe.wait_ge(negm_ready, a.total(1, 1))
                            if a.plus(2).after(1) and a.plus(2).exists():
                                pe.wait_ge(qf_ready, a.plus(2).total(2, 2))
                            for it in range(2):
                                i = nc.tensor.transpose(P_TOK[0:HEADS, HALF * it:HALF * it + HALF].bitcast(F32R),
                                                        negm[:, it, :].bitcast(F32R), identr[0:HALF, 0:HALF])
                            i.then_inc(m_turned, 1)
                        a = t.plus(5)
                        for step in (range(u - 1, u + 1) if a.exists() and u % 2 else ()):
                            if step == 0:
                                pe.wait_ge(x_loaded[a.place % 2], a.turn(2, 16 * SPLIT * CH))
                                if a.after(1):
                                    pe.wait_ge(h_ready, a.total(1, 0))
                            i = nc.tensor.matmul(
                                P_EMB[:, 0:TOK].rearrange("p (y x) -> p y x", y=GRID), w_embed[:, step, :],
                                xin[a.place % 2][:, :, step:IMG - PATCH + step + 1:PATCH], start=(step == 0),
                                stop=(step == STEP - 1))
                            if step == STEP - 1:
                                i.then_inc(embedded, 1)

                period_range(pe, period, 5, 1)

        phase1.close()
        lifetime[0] = ctx
        UN = 4
        NP = B // 2
        yrel = [sb(f"yrel{k}", [E, 2, TOK]) for k in range(2)]
        hin = [sb(f"hin{k}", [E, 2, TOK]) for k in range(2)]
        x2 = [sb(f"x2{k}", [E, 2, TOK]) for k in range(2)]
        st2 = sb("st2", [HALF, 4, 6])
        mv2 = sb("mv2", [HALF, 4, 2])
        ve2 = sb("ve2", [HALF, 4])
        rs2 = sb("rs2", [HALF, 4])
        ln = [sb(f"ln{k}", [HALF, 4, E]) for k in range(2)]
        res = [sb(f"res{k}", [HALF, 4, E]) for k in range(UN)]
        dT = sb("dT", [E, 2 * HALF])
        z = sb("z", [HALF, 2, E])
        zT = [sb(f"zT{k}", [E, 2 * HALF]) for k in range(UN)]
        hid = [sb(f"hid{k}", [128, HT, 2 * HALF]) for k in range(2)]
        fin = [sb(f"fin{k}", [HALF, 4, E]) for k in range(2)]
        Q_T, Q_Z, Q_H, Q_D, Q_F = bank[0:2], bank[2], bank[4:6], bank[6], bank[7]

        h_back = [sem(f"h_back{k}") for k in range(2)]
        stored = [sem(f"stored{k}") for k in range(2)]
        rel_ready = sem("rel_ready")
        x2_ready = sem("x2_ready")
        x2_turned = sem("x2_turned")
        st2_in = sem("st2_in")
        mv2_ready = sem("mv2_ready")
        ve2_ready = sem("ve2_ready")
        rs2_ready = sem("rs2_ready")
        ln_ready = sem("ln_ready")
        res_ready = sem("res_ready")
        z_ready = sem("z_ready")
        z_turned = sem("z_turned")
        zT_ready = sem("zT_ready")
        hid_out = sem("hid_out")
        hid_ready = sem("hid_ready")
        ffn_out = sem("ffn_out")
        dT_ready = sem("dT_ready")
        d_turned = sem("d_turned")
        fin_ready = sem("fin_ready")

        class Pair(Image):

            def __init__(self, block, place):
                self.fixed = isinstance(block, int)
                self.block = block + place // UN
                self.place = place % UN
                self.index = self.block * UN + self.place

            @property
            def odd(self):
                return self.place % 2

            def plus(self, d):
                return Pair(self.block, self.place + d)

            def exists(self, count=NP):
                return not self.fixed or 0 <= self.index < count

            def total(self, per, c):
                return self.block * (UN * per) + (self.place * per + c)

            def turn(self, slots, per):
                return self.block * (UN // slots * per) + (self.place // slots + 1) * per

        def pair_range(eng, period, lead):
            for t in range(-lead, UN):
                period(Pair(0, t))
            with eng.Fori(1, NP // UN - 2) as i:
                for k in range(UN):
                    period(Pair(i, k))
            for t in range(NP - 2 * UN, NP + 1):
                period(Pair(0, t))

        h_pairs = h_dram.rearrange("b (q r) e t -> (b q) e r t", r=2)
        out_pairs = out.rearrange("(q r) (p d) e -> q p r (d e)", r=2, d=2)

        with nc.Block() as block:

            @block.sync
            def _(sp):
                def period(t):
                    a = t.plus(6)
                    if a.exists():
                        if a.after(2):
                            sp.wait_ge(x2_ready, a.plus(-2).total(1, 1))
                        settle(sp)
                        sp.dma_start(hin[a.odd][:, :, :], h_pairs[a.index]).then_inc(h_back[a.odd], 16)
                    a = t.plus(-1)
                    if a.exists():
                        sp.wait_ge(fin_ready, a.total(1, 1))
                        settle(sp)
                        sp.dma_start(out_pairs[a.index],
                                     fin[a.odd][:, :, :].rearrange("p (r d) e -> p r (d e)", r=2))\
                            .then_inc(stored[a.odd], 16)

                pair_range(sp, period, 6)
                for k in range(2):
                    sp.wait_ge(stored[k], 16 * (NP // 2))

            @block.vector
            def _(dve):
                nc.vector.bn_aggr(bn[:, 0:2], ostats[:, :]).then_inc(bn_ready, 1)
                dve.wait_ge(bn_ready, 3)
                nc.vector.tensor_tensor(bn[:, 3:4], bn[:, 2:3], gam[:, :], ALU.mult).then_inc(bn_ready, 1)
                dve.wait_ge(bn_ready, 4)
                nc.vector.tensor_tensor(bn[:, 4:5], bn[:, 0:1], bn[:, 3:4], ALU.mult).then_inc(bn_ready, 1)
                dve.wait_ge(bn_ready, 5)
                nc.vector.tensor_tensor(bn[:, 5:6], bet[:, :], bn[:, 4:5], ALU.subtract).then_inc(bn_ready, 1)

                def tiles(a):
                    return Q_T[a.odd][0:HALF, :].rearrange("p (n e) -> p n e", n=4)

                def period(t):
                    a = t.plus(3)
                    if a.exists():
                        dve.wait_ge(x2_turned, a.total(1, 1))
                        for n in range(4):
                            nc.vector.bn_stats(st2[:, n, :], tiles(a)[:, n, :]).then_inc(st2_in, 1)
                        dve.wait_ge(st2_in, a.total(4, 4))
                        if a.after(1):
                            dve.wait_ge(ln_ready, a.total(4, 0))
                        settle(dve)
                        for n in range(4):
                            nc.vector.bn_aggr(mv2[:, n, :], st2[:, n, :]).then_inc(mv2_ready, 1)
                    a = t.plus(-1)
                    if a.exists():
                        dve.wait_ge(d_turned, a.total(1, 1))
                        if a.after(2):
                            dve.wait_ge(stored[a.odd], a.plus(-2).turn(2, 16))
                        nc.vector.tensor_tensor(
                            fin[a.odd][:, :, :].rearrange("p (r d) e -> p r d e", r=2),
                            res[a.place][:, :, :].rearrange("p (r d) e -> p r d e", r=2),
                            Q_F[0:HALF, 0:2 * E].rearrange("p (r e) -> p r e", r=2).unsqueeze(2)
                            .to_broadcast([HALF, 2, 2, E]), ALU.add).then_inc(fin_ready, 1)
                    a = t.plus(2)
                    if a.exists():
                        dve.wait_ge(ln_ready, a.total(4, 4))
                        nc.vector.tensor_tensor(res[a.place][:, :, :], tiles(a), ln[a.odd][:, :, :], ALU.add)\
                            .then_inc(res_ready, 1)
                    a = t.plus(3)
                    if a.exists():
                        dve.wait_ge(rs2_ready, a.total(1, 1))
                        if a.after(2):
                            dve.wait_ge(z_ready, a.plus(-2).total(1, 1))
                        for n in range(4):
                            nc.vector.tensor_scalar(ln[a.odd][:, n, :], tiles(a)[:, n, :], mv2[:, n, 0:1],
                                                    rs2[:, n:n + 1], ALU.subtract, ALU.mult).then_inc(ln_ready, 1)

                pair_range(dve, period, 6)

            @block.gpsimd
            def _(pool):
                pool.wait_ge(bn_ready, 1)
                settle(pool)
                pool.tensor_scalar(bn[:, 4:5], bn[:, 1:2], EPS, None, ALU.add).then_inc(bn_ready, 1)
                pool.wait_ge(bn_ready, 2)
                pool.tensor_tensor(bn[:, 2:3], bn[:, 4:5], minus_half[:, 0:1], ALU.pow).then_inc(bn_ready, 1)

                def period(t):
                    a = t.plus(3)
                    if a.exists():
                        pool.wait_ge(mv2_ready, a.total(4, 4))
                        if a.after(1):
                            pool.wait_ge(ln_ready, a.total(4, 0))
                        settle(pool)
                        pool.tensor_scalar(ve2[:, :], mv2[:, :, 1], EPS, None, ALU.add).then_inc(ve2_ready, 1)
                        pool.wait_ge(ve2_ready, a.total(1, 1))
                        pool.tensor_tensor(rs2[:, :], ve2[:, :], minus_half[0:HALF, :], ALU.pow)\
                            .then_inc(rs2_ready, 1)
                    a = t.plus(5)
                    if a.exists():
                        pool.wait_ge(rel_ready, a.total(1, 1))
                        pool.wait_ge(h_back[a.odd], a.turn(2, 16))
                        if a.after(2):
                            pool.wait_ge(x2_turned, a.plus(-2).total(1, 1))
                        pool.tensor_tensor(x2[a.odd][:, :, :], yrel[a.odd][:, :, :], hin[a.odd][:, :, :],
                                           ALU.add).then_inc(x2_ready, 1)
                    a = t.plus(3)
                    if a.exists():
                        pool.wait_ge(ln_ready, a.total(4, 4))
                        if a.after(1):
                            pool.wait_ge(z_turned, a.total(1, 0))
                        pool.tensor_tensor(z[:, :, :], ln[a.odd][:, 0::2, :], ln[a.odd][:, 1::2, :],
                                           ALU.add).then_inc(z_ready, 1)

                pair_range(pool, period, 6)

            @block.scalar
            def _(act):
                act.wait_ge(bn_ready, 6)

                def period(t):
                    a = t.plus(5)
                    if a.exists():
                        if a.after(2):
                            act.wait_ge(x2_ready, a.plus(-2).total(1, 1))
                        nc.scalar.activation(yrel[a.odd][:, :, :].rearrange("p r t -> p (r t)"),
                                             oT[:, bass.ds(a.index * (2 * TOK), 2 * TOK)], ACT.Relu,
                                             bias=bn[:, 5:6], scale=bn[:, 3:4]).then_inc(rel_ready, 1)
                    if t.exists():
                        act.wait_ge(ffn_out, t.total(1, 1))
                        if t.after(1):
                            act.wait_ge(d_turned, t.total(1, 0))
                        nc.scalar.activation(dT[:, :], Q_D[:, 0:2 * HALF], ACT.Identity, bias=b_ffn2[:, 0:1])\
                            .then_inc(dT_ready, 1)
                    a = t.plus(2)
                    if a.exists():
                        act.wait_ge(z_turned, a.total(1, 1))
                        if a.after(4):
                            act.wait_ge(ffn_out, a.plus(-4).total(1, 1))
                        nc.scalar.activation(zT[a.place][:, :], Q_Z[:, 0:2 * HALF], ACT.Copy).then_inc(zT_ready, 1)
                    a = t.plus(1)
                    if a.exists():
                        for k in range(HT):
                            act.wait_ge(hid_out, a.total(2, k // 2 + 1))
                            nc.scalar.activation(hid[a.odd][:, k, :],
                                                 Q_H[k // 2][:, TOK * (k % 2):TOK * (k % 2) + TOK], ACT.Gelu,
                                                 bias=b_ffn1[:, k:k + 1]).then_inc(hid_ready, 1)

                pair_range(act, period, 6)

            @block.tensor
            def _(pe):
                def period(t):
                    a = t.plus(3)
                    if a.exists():
                        pe.wait_ge(x2_ready, a.total(1, 1))
                        if a.after(2):
                            pe.wait_ge(res_ready, a.plus(-2).total(1, 1))
                        for r in range(2):
                            for d in range(2):
                                n = 2 * r + d
                                i = nc.tensor.transpose(Q_T[a.odd][0:HALF, E * n:E * n + E],
                                                        x2[a.odd][:, r, d::2], ident[:, :])
                        i.then_inc(x2_turned, 1)
                    a = t.plus(-1)
                    if a.exists():
                        pe.wait_ge(dT_ready, a.total(1, 1))
                        if a.after(1):
                            pe.wait_ge(fin_ready, a.total(1, 0))
                        for r in range(2):
                            i = nc.tensor.transpose(Q_F[0:HALF, E * r:E * r + E], dT[:, HALF * r:HALF * r + HALF],
                                                    ident[:, :])
                        i.then_inc(d_turned, 1)
                    if t.exists():
                        if t.after(1):
                            pe.wait_ge(dT_ready, t.total(1, 0))
                        nc.tensor.matmul(Q_D[:, 0:2 * HALF], pairsum[:, :], zT[t.place][:, :],
                                         start=True, stop=False)
                        for k in range(HT):
                            pe.wait_ge(hid_ready, t.total(HT, k + 1))
                            i = nc.tensor.matmul(Q_D[:, 0:2 * HALF], w_ffn2[:, k, :], hid[t.odd][:, k, :],
                                                 start=False, stop=(k == HT - 1))
                        i.then_inc(ffn_out, 1)
                    a = t.plus(2)
                    if a.exists():
                        pe.wait_ge(z_ready, a.total(1, 1))
                        if a.after(1):
                            pe.wait_ge(zT_ready, a.total(1, 0))
                        for r in range(2):
                            i = nc.tensor.transpose(Q_Z[:, HALF * r:HALF * r + HALF], z[:, r, :],
                                                    ident[0:HALF, 0:HALF])
                        i.then_inc(z_turned, 1)
                    a = t.plus(1)
                    if a.exists():
                        pe.wait_ge(zT_ready, a.total(1, 1))
                        for k in range(HT):
                            if k % 2 == 0 and a.after(1):
                                pe.wait_ge(hid_ready, a.total(HT, k + 2 - HT))
                            i = nc.tensor.matmul(Q_H[k // 2][:, TOK * (k % 2):TOK * (k % 2) + TOK],
                                                 w_ffn1[:, 128 * k:128 * k + 128], zT[a.place][:, :],
                                                 start=True, stop=True)
                            if k % 2:
                                i.then_inc(hid_out, 1)

                pair_range(pe, period, 6)


_INS = ['x', 'L0_tok_w', 'L0_tok_b', 'L0_attn_wq', 'L0_attn_wk', 'L0_attn_wv', 'L0_attn_wo', 'L0_attn_gamma',
        'L0_attn_beta', 'L0_ffn_fc1_w', 'L0_ffn_fc1_b', 'L0_ffn_fc2_w', 'L0_ffn_fc2_b']


def shape_constants():
    ident = np.eye(E, dtype=np.float32)
    center = (np.eye(E) - 1.0 / E).astype(np.float32)
    heads = np.kron(np.eye(HEADS), np.full((C, C), DH ** -0.5)).astype(np.float32)
    n, m = E // 2, E
    pos = np.linspace(0.0, 1.0, m, dtype=np.float32) * np.float32(n - 1)
    i0 = np.clip(np.floor(pos).astype(np.int64), 0, n - 2)
    w = pos - i0.astype(np.float32)
    interp = np.zeros((m, n), np.float32)
    interp[np.arange(m), i0] = 1 - w
    interp[np.arange(m), i0 + 1] = w
    interp = np.repeat(0.5 * interp, 2, axis=1)
    pair = np.kron(np.eye(n), np.full((2, 2), -0.25)).astype(np.float32)
    return {"c_ident": ident, "c_center": center, "c_heads": heads,
            "c_interp": np.ascontiguousarray(interp, np.float32), "c_pair": pair}


def kernel(**inputs):
    import concourse.bacc as _bacc
    from concourse.bass_utils import run_bass_kernel_spmd as _run

    nc = _bacc.Bacc("TRN2", target_bir_lowering=False, num_devices=1)
    arrays, args = {}, []
    for name, a in [(n, inputs[n]) for n in _INS] + list(shape_constants().items()):
        a = np.ascontiguousarray(a)
        arrays[f"in_{name}"] = a
        args.append(nc.dram_tensor(f"in_{name}", a.shape, mybir.dt.from_np(a.dtype), kind="ExternalInput").ap())
    out = nc.dram_tensor("out_0", (B, TOK, E), F32, kind="ExternalOutput").ap()
    vit_layer(nc, *args, out)
    r = _run(nc, [arrays], core_ids=[0])
    return r.results[0]["out_0"]
```
